# Optimizing a Trainium2 kernel written in Bass

```python
import numpy as np
import jax
import jax.numpy as jnp

def _softmax(x, axis=-1):
    return jax.nn.softmax(x, axis=axis)

def _gelu(x):
    return jax.nn.gelu(x, approximate=True)

def _silu(x):
    return jax.nn.silu(x)

def _sigmoid(x):
    return jax.nn.sigmoid(x)

def _layernorm(x, axis=-1, eps=1e-05):
    m = jnp.mean(x, axis=axis, keepdims=True)
    v = jnp.var(x, axis=axis, keepdims=True)
    return (x - m) / jnp.sqrt(v + eps)

def _scatter_add(tgt, idx, src, axis=0):
    return tgt.at[idx].add(src)

def _segment_sum(src, seg, n):
    return jax.ops.segment_sum(src, seg, n)
kernel_name = 'mk_xattn_seq_d4_seqx_r8_5eef44'

def setup_inputs(seed: int=0):
    np.random.seed(seed)
    _w = jnp.asarray

    def _rec_inputs():
        import jax
        import jax.numpy as jnp
        _rk = jax.random.key(seed)
        x = -0.0003929 + 0.9999 * jax.random.normal(jax.random.fold_in(_rk, 1), (4, 256, 256), jnp.float32)
        _lenS = 256 - jax.random.randint(jax.random.fold_in(_rk, 7), (4,), 0, max(1, 256 // 4) + 1, jnp.int32)
        _lenS2 = 1601 - jax.random.randint(jax.random.fold_in(_rk, 8), (4,), 0, max(1, 1601 // 4) + 1, jnp.int32)
        _ctx_1024P = jax.random.normal(jax.random.fold_in(_rk, 11), (4, 16, 128), jnp.float32)
        _ctx_1024c = jax.random.dirichlet(jax.random.fold_in(_rk, 511), 0.3 * jnp.ones((16,), jnp.float32), (4, 1601))
        _ctx_1024t = jnp.einsum('bsk,bkd->bsd', _ctx_1024c, _ctx_1024P)
        _ctx_1024t = _ctx_1024t * jax.lax.rsqrt(jnp.mean(jnp.square(_ctx_1024t)) + 1e-12) * 0.953939
        ctx_1024 = 0.00191187 + 0.999416 * (_ctx_1024t + 0.3 * jax.random.normal(jax.random.fold_in(_rk, 611), (4, 1601, 128), jnp.float32))
        pos_1xS = jnp.broadcast_to(jnp.arange(256, dtype=jnp.int32), (1, 256))
        _validS = jnp.arange(256)[None, :] < _lenS[:, None]
        _validS2 = jnp.arange(1601)[None, :] < _lenS2[:, None]
        _causal = jnp.tril(jnp.ones((256, 256), dtype=bool))
        mask_BxS2_bk0 = jnp.logical_not(jnp.broadcast_to(_validS2[:, :], (4, 1601)))
        mask_BxS_ik0 = jnp.where(jnp.broadcast_to(_validS[:, :], (4, 256)), 0, 1).astype(jnp.int32)
        return (x, ctx_1024, pos_1xS, mask_BxS2_bk0, mask_BxS_ik0)
    x, ctx_1024, pos_1xS, mask_BxS2_bk0, mask_BxS_ik0 = _rec_inputs()

    def _L0_xattn_setup():
        import jax, jax.numpy as jnp
        import numpy as np
        DIM = 256
        DIM_MEDIA = 128
        HEADS = 16
        DIM_HEAD = 64
        INNER = HEADS * DIM_HEAD
        FF_INNER = 4 * DIM
        B, N_TOK, N_LAT = (4, 256, 64)
        EPS = 1e-05

        def layernorm(x, g, b):
            mu = jnp.mean(x, axis=-1, keepdims=True)
            var = jnp.var(x, axis=-1, keepdims=True)
            return (x - mu) * jax.lax.rsqrt(var + EPS) * g + b
        key = jax.random.key(seed)
        ks = jax.random.split(key, 12)
        x = jax.random.normal(ks[0], (B, N_TOK, DIM), dtype=jnp.float32)
        media = jax.random.normal(ks[1], (B, N_LAT, DIM_MEDIA), dtype=jnp.float32)
        media_mask = jax.random.randint(ks[2], (B, N_LAT), 0, 2).astype(bool)
        media_mask = media_mask.at[:, 0].set(True)
        s = lambda d: 1.0 / np.sqrt(d)
        Wq = jax.random.normal(ks[3], (DIM, INNER), dtype=jnp.float32) * s(DIM)
        Wkv = jax.random.normal(ks[4], (DIM_MEDIA, 2 * INNER), dtype=jnp.float32) * s(DIM_MEDIA)
        Wo = jax.random.normal(ks[5], (INNER, DIM), dtype=jnp.float32) * s(INNER)
        W1 = jax.random.normal(ks[6], (DIM, FF_INNER), dtype=jnp.float32) * s(DIM)
        W2 = jax.random.normal(ks[7], (FF_INNER, DIM), dtype=jnp.float32) * s(FF_INNER)
        return {'x': x, 'media': media, 'media_mask': media_mask, 'ln_q_g': jnp.ones((DIM,), jnp.float32), 'ln_q_b': jnp.zeros((DIM,), jnp.float32), 'Wq': Wq, 'Wkv': Wkv, 'Wo': Wo, 'attn_gate': jax.random.normal(ks[8], (1,), jnp.float32) * 0.5, 'ln_ff_g': jnp.ones((DIM,), jnp.float32), 'ln_ff_b': jnp.zeros((DIM,), jnp.float32), 'W1': W1, 'W2': W2, 'ff_gate': jax.random.normal(ks[9], (1,), jnp.float32) * 0.5}
    _L0_xattn_all = _L0_xattn_setup()
    _L0_xattn_in = {k: v for k, v in _L0_xattn_all.items() if k in ('ln_q_g', 'ln_q_b', 'Wq', 'Wkv', 'Wo', 'attn_gate', 'ln_ff_g', 'ln_ff_b', 'W1', 'W2', 'ff_gate')}
    del _L0_xattn_all

    def _L1_xattn_setup():
        import jax, jax.numpy as jnp
        import numpy as np
        EPS = 1e-06

        def _rmsnorm(x, w):
            var = jnp.mean(jnp.square(x), axis=-1, keepdims=True)
            return x * jax.lax.rsqrt(var + EPS) * w
        key = jax.random.key(seed)
        ks = jax.random.split(key, 6)
        B, N, M = (4, 512, 256)
        d_model, memory_dim = (256, 128)
        hidden_states = jax.random.normal(ks[0], (B, N, d_model), dtype=jnp.float32)
        memory = jax.random.normal(ks[1], (B, M, memory_dim), dtype=jnp.float32)
        W_mem = jax.random.normal(ks[2], (d_model, memory_dim), dtype=jnp.float32) / np.sqrt(memory_dim)
        W_gate = jax.random.normal(ks[3], (d_model, 2 * d_model), dtype=jnp.float32) / np.sqrt(2 * d_model)
        b_gate = jax.random.normal(ks[4], (d_model,), dtype=jnp.float32) * 0.01
        norm_w = jnp.ones((d_model,), dtype=jnp.float32)
        return {'hidden_states': hidden_states, 'memory': memory, 'W_mem': W_mem, 'W_gate': W_gate, 'b_gate': b_gate, 'norm_w': norm_w}
    _L1_xattn_all = _L1_xattn_setup()
    _L1_xattn_in = {k: v for k, v in _L1_xattn_all.items() if k in ('W_mem', 'W_gate', 'b_gate', 'norm_w')}
    del _L1_xattn_all

    def _L2_xattn_setup():
        import jax, jax.numpy as jnp
        import numpy as np
        H = 256
        NH = 16
        HD = H // NH
        CH = 128
        CC = 128
        CHD = CC // NH
        I = 688
        B = 2
        L = 256
        LE = 128
        EPS = 1e-06

        def rms_norm(x, w):
            xf = x.astype(jnp.float32)
            var = jnp.mean(xf * xf, axis=-1, keepdims=True)
            return (w * (xf * jax.lax.rsqrt(var + EPS))).astype(x.dtype)

        def expert_mask(tt):
            vm = jnp.zeros(tt.shape, dtype=bool)
            vm = vm.at[:, :-1].set((tt[:, :-1] == 1) & (tt[:, 1:] == 1))
            return vm

        def rotate_half(x):
            d = x.shape[-1] // 2
            return jnp.concatenate([-x[..., d:], x[..., :d]], axis=-1)

        def apply_rotary(q, k, position_ids, seq_len):
            inv = 1.0 / 10000.0 ** (jnp.arange(0, HD, 2, dtype=jnp.float32) / HD)
            t = jnp.arange(seq_len, dtype=jnp.float32)
            freqs = jnp.outer(t, inv)
            emb = jnp.concatenate([freqs, freqs], axis=-1)
            cos = jnp.cos(emb)[position_ids][:, None].astype(q.dtype)
            sin = jnp.sin(emb)[position_ids][:, None].astype(q.dtype)
            return (q * cos + rotate_half(q) * sin, k * cos + rotate_half(k) * sin)

        def sdpa(q, k, v, causal):
            scale = 1.0 / np.sqrt(q.shape[-1])
            scores = jnp.einsum('bhqd,bhkd->bhqk', q * scale, k)
            if causal:
                mask = jnp.tril(jnp.ones((q.shape[-2], k.shape[-2]), dtype=bool))
                scores = jnp.where(mask, scores, jnp.finfo(jnp.float32).min)
            p = jax.nn.softmax(scores.astype(jnp.float32), axis=-1).astype(q.dtype)
            return jnp.einsum('bhqk,bhkd->bhqd', p, v)

        def heads(x, nh, hd):
            b, l, _ = x.shape
            return x.reshape(b, l, nh, hd).transpose(0, 2, 1, 3)
        key = jax.random.key(seed)
        ks = jax.random.split(key, 20)
        s = 0.02
        f32 = jnp.float32
        return {'hidden_states': jax.random.normal(ks[0], (B, L, H), f32), 'encoder_outputs': jax.random.normal(ks[1], (B, LE, CH), f32), 'token_type_ids': jax.random.randint(ks[2], (B, L), 0, 2, jnp.int32), 'position_ids': jnp.arange(L, dtype=jnp.int32)[None, :], 'ln_in_w': jnp.ones((H,), f32), 'ln_post_attn_w': jnp.ones((H,), f32), 'ln_post_cross_w': jnp.ones((H,), f32), 'v_qkv': jax.random.normal(ks[3], (H, 3 * H), f32) * s, 'l_qkv': jax.random.normal(ks[4], (H, 3 * H), f32) * s, 'v_dense': jax.random.normal(ks[5], (H, H), f32) * s, 'l_dense': jax.random.normal(ks[6], (H, H), f32) * s, 'cq_w': jax.random.normal(ks[7], (H, CC), f32) * s, 'ckv_w': jax.random.normal(ks[8], (CH, 2 * CC), f32) * s, 'cdense_w': jax.random.normal(ks[9], (CC, H), f32) * s, 'v_gate': jax.random.normal(ks[10], (H, I), f32) * s, 'v_up': jax.random.normal(ks[11], (H, I), f32) * s, 'v_down': jax.random.normal(ks[12], (I, H), f32) * s, 'l_gate': jax.random.normal(ks[13], (H, I), f32) * s, 'l_up': jax.random.normal(ks[14], (H, I), f32) * s, 'l_down': jax.random.normal(ks[15], (I, H), f32) * s}
    _L2_xattn_all = _L2_xattn_setup()
    _L2_xattn_in = {k: v for k, v in _L2_xattn_all.items() if k in ('ln_in_w', 'ln_post_attn_w', 'ln_post_cross_w', 'v_qkv', 'l_qkv', 'v_dense', 'l_dense', 'cq_w', 'ckv_w', 'cdense_w', 'v_gate', 'v_up', 'v_down', 'l_gate', 'l_up', 'l_down')}
    del _L2_xattn_all

    def _L3_xattn_setup():
        import jax, jax.numpy as jnp
        import numpy as np
        EPS = 1e-06

        def _rmsnorm(x, w):
            var = jnp.mean(jnp.square(x), axis=-1, keepdims=True)
            return x * jax.lax.rsqrt(var + EPS) * w
        key = jax.random.key(seed)
        ks = jax.random.split(key, 6)
        B, N, M = (4, 512, 256)
        d_model, memory_dim = (256, 128)
        hidden_states = jax.random.normal(ks[0], (B, N, d_model), dtype=jnp.float32)
        memory = jax.random.normal(ks[1], (B, M, memory_dim), dtype=jnp.float32)
        W_mem = jax.random.normal(ks[2], (d_model, memory_dim), dtype=jnp.float32) / np.sqrt(memory_dim)
        W_gate = jax.random.normal(ks[3], (d_model, 2 * d_model), dtype=jnp.float32) / np.sqrt(2 * d_model)
        b_gate = jax.random.normal(ks[4], (d_model,), dtype=jnp.float32) * 0.01
        norm_w = jnp.ones((d_model,), dtype=jnp.float32)
        return {'hidden_states': hidden_states, 'memory': memory, 'W_mem': W_mem, 'W_gate': W_gate, 'b_gate': b_gate, 'norm_w': norm_w}
    _L3_xattn_all = _L3_xattn_setup()
    _L3_xattn_in = {k: v for k, v in _L3_xattn_all.items() if k in ('W_mem', 'W_gate', 'b_gate', 'norm_w')}
    del _L3_xattn_all
    return {'x': x, 'ctx_1024': ctx_1024, 'pos_1xS': pos_1xS, 'mask_BxS2_bk0': mask_BxS2_bk0, 'mask_BxS_ik0': mask_BxS_ik0, 'L0_xattn_ln_q_g': _L0_xattn_in['ln_q_g'], 'L0_xattn_ln_q_b': _L0_xattn_in['ln_q_b'], 'L0_xattn_Wq': _L0_xattn_in['Wq'], 'L0_xattn_Wkv': _L0_xattn_in['Wkv'], 'L0_xattn_Wo': _L0_xattn_in['Wo'], 'L0_xattn_attn_gate': _L0_xattn_in['attn_gate'], 'L0_xattn_ln_ff_g': _L0_xattn_in['ln_ff_g'], 'L0_xattn_ln_ff_b': _L0_xattn_in['ln_ff_b'], 'L0_xattn_W1': _L0_xattn_in['W1'], 'L0_xattn_W2': _L0_xattn_in['W2'], 'L0_xattn_ff_gate': _L0_xattn_in['ff_gate'], 'L1_xattn_W_mem': _L1_xattn_in['W_mem'], 'L1_xattn_W_gate': _L1_xattn_in['W_gate'], 'L1_xattn_b_gate': _L1_xattn_in['b_gate'], 'L1_xattn_norm_w': _L1_xattn_in['norm_w'], 'L2_xattn_ln_in_w': _L2_xattn_in['ln_in_w'], 'L2_xattn_ln_post_attn_w': _L2_xattn_in['ln_post_attn_w'], 'L2_xattn_ln_post_cross_w': _L2_xattn_in['ln_post_cross_w'], 'L2_xattn_v_qkv': _L2_xattn_in['v_qkv'], 'L2_xattn_l_qkv': _L2_xattn_in['l_qkv'], 'L2_xattn_v_dense': _L2_xattn_in['v_dense'], 'L2_xattn_l_dense': _L2_xattn_in['l_dense'], 'L2_xattn_cq_w': _L2_xattn_in['cq_w'], 'L2_xattn_ckv_w': _L2_xattn_in['ckv_w'], 'L2_xattn_cdense_w': _L2_xattn_in['cdense_w'], 'L2_xattn_v_gate': _L2_xattn_in['v_gate'], 'L2_xattn_v_up': _L2_xattn_in['v_up'], 'L2_xattn_v_down': _L2_xattn_in['v_down'], 'L2_xattn_l_gate': _L2_xattn_in['l_gate'], 'L2_xattn_l_up': _L2_xattn_in['l_up'], 'L2_xattn_l_down': _L2_xattn_in['l_down'], 'L3_xattn_W_mem': _L3_xattn_in['W_mem'], 'L3_xattn_W_gate': _L3_xattn_in['W_gate'], 'L3_xattn_b_gate': _L3_xattn_in['b_gate'], 'L3_xattn_norm_w': _L3_xattn_in['norm_w']}

def reference(x, ctx_1024, pos_1xS, mask_BxS2_bk0, mask_BxS_ik0, L0_xattn_ln_q_g, L0_xattn_ln_q_b, L0_xattn_Wq, L0_xattn_Wkv, L0_xattn_Wo, L0_xattn_attn_gate, L0_xattn_ln_ff_g, L0_xattn_ln_ff_b, L0_xattn_W1, L0_xattn_W2, L0_xattn_ff_gate, L1_xattn_W_mem, L1_xattn_W_gate, L1_xattn_b_gate, L1_xattn_norm_w, L2_xattn_ln_in_w, L2_xattn_ln_post_attn_w, L2_xattn_ln_post_cross_w, L2_xattn_v_qkv, L2_xattn_l_qkv, L2_xattn_v_dense, L2_xattn_l_dense, L2_xattn_cq_w, L2_xattn_ckv_w, L2_xattn_cdense_w, L2_xattn_v_gate, L2_xattn_v_up, L2_xattn_v_down, L2_xattn_l_gate, L2_xattn_l_up, L2_xattn_l_down, L3_xattn_W_mem, L3_xattn_W_gate, L3_xattn_b_gate, L3_xattn_norm_w):
    import jax
    import jax.numpy as jnp

    def _L0_xattn_ref(x, media, media_mask, ln_q_g, ln_q_b, Wq, Wkv, Wo, attn_gate, ln_ff_g, ln_ff_b, W1, W2, ff_gate):
        import jax, jax.numpy as jnp
        import numpy as np
        DIM = 256
        DIM_MEDIA = 128
        HEADS = 16
        DIM_HEAD = 64
        INNER = HEADS * DIM_HEAD
        FF_INNER = 4 * DIM
        B, N_TOK, N_LAT = (4, 256, 64)
        EPS = 1e-05

        def layernorm(x, g, b):
            mu = jnp.mean(x, axis=-1, keepdims=True)
            var = jnp.var(x, axis=-1, keepdims=True)
            return (x - mu) * jax.lax.rsqrt(var + EPS) * g + b
        scale = DIM_HEAD ** (-0.5)
        qn = layernorm(x, ln_q_g, ln_q_b)
        q = qn @ Wq * scale
        kv = media @ Wkv
        k, v = jnp.split(kv, 2, axis=-1)
        split_heads = lambda t: t.reshape(t.shape[0], t.shape[1], HEADS, DIM_HEAD).transpose(0, 2, 1, 3)
        q, k, v = (split_heads(q), split_heads(k), split_heads(v))
        sim = jnp.einsum('bhid,bhjd->bhij', q, k)
        neg_inf = jnp.finfo(sim.dtype).min
        sim = jnp.where(media_mask[:, None, None, :], sim, neg_inf)
        attn = jax.nn.softmax(sim, axis=-1)
        out = jnp.einsum('bhij,bhjd->bhid', attn, v)
        out = out.transpose(0, 2, 1, 3).reshape(x.shape[0], x.shape[1], INNER)
        attn_out = out @ Wo
        x = x + jnp.tanh(attn_gate) * attn_out
        h = layernorm(x, ln_ff_g, ln_ff_b)
        h = jax.nn.gelu(h @ W1, approximate=False) @ W2
        x = x + jnp.tanh(ff_gate) * h
        return x

    def _L1_xattn_ref(hidden_states, memory, W_mem, W_gate, b_gate, norm_w):
        import jax, jax.numpy as jnp
        import numpy as np
        EPS = 1e-06

        def _rmsnorm(x, w):
            var = jnp.mean(jnp.square(x), axis=-1, keepdims=True)
            return x * jax.lax.rsqrt(var + EPS) * w
        D = hidden_states.shape[-1]
        memory_proj = jnp.einsum('bme,de->bmd', memory, W_mem)
        scores = jnp.einsum('bnd,bmd->bnm', hidden_states, memory_proj) / jnp.sqrt(jnp.float32(D))
        attn = jax.nn.softmax(scores, axis=-1)
        memory_context = jnp.einsum('bnm,bmd->bnd', attn, memory_proj)
        gate_input = jnp.concatenate([hidden_states, memory_context], axis=-1)
        gate = jax.nn.sigmoid(jnp.einsum('bnf,df->bnd', gate_input, W_gate) + b_gate)
        fused = hidden_states + gate * memory_context
        return _rmsnorm(fused, norm_w)

    def _L2_xattn_ref(hidden_states, encoder_outputs, token_type_ids, position_ids, ln_in_w, ln_post_attn_w, ln_post_cross_w, v_qkv, l_qkv, v_dense, l_dense, cq_w, ckv_w, cdense_w, v_gate, v_up, v_down, l_gate, l_up, l_down):
        import jax, jax.numpy as jnp
        import numpy as np
        H = 256
        NH = 16
        HD = H // NH
        CH = 128
        CC = 128
        CHD = CC // NH
        I = 688
        B = 2
        L = 256
        LE = 128
        EPS = 1e-06

        def rms_norm(x, w):
            xf = x.astype(jnp.float32)
            var = jnp.mean(xf * xf, axis=-1, keepdims=True)
            return (w * (xf * jax.lax.rsqrt(var + EPS))).astype(x.dtype)

        def expert_mask(tt):
            vm = jnp.zeros(tt.shape, dtype=bool)
            vm = vm.at[:, :-1].set((tt[:, :-1] == 1) & (tt[:, 1:] == 1))
            return vm

        def rotate_half(x):
            d = x.shape[-1] // 2
            return jnp.concatenate([-x[..., d:], x[..., :d]], axis=-1)

        def apply_rotary(q, k, position_ids, seq_len):
            inv = 1.0 / 10000.0 ** (jnp.arange(0, HD, 2, dtype=jnp.float32) / HD)
            t = jnp.arange(seq_len, dtype=jnp.float32)
            freqs = jnp.outer(t, inv)
            emb = jnp.concatenate([freqs, freqs], axis=-1)
            cos = jnp.cos(emb)[position_ids][:, None].astype(q.dtype)
            sin = jnp.sin(emb)[position_ids][:, None].astype(q.dtype)
            return (q * cos + rotate_half(q) * sin, k * cos + rotate_half(k) * sin)

        def sdpa(q, k, v, causal):
            scale = 1.0 / np.sqrt(q.shape[-1])
            scores = jnp.einsum('bhqd,bhkd->bhqk', q * scale, k)
            if causal:
                mask = jnp.tril(jnp.ones((q.shape[-2], k.shape[-2]), dtype=bool))
                scores = jnp.where(mask, scores, jnp.finfo(jnp.float32).min)
            p = jax.nn.softmax(scores.astype(jnp.float32), axis=-1).astype(q.dtype)
            return jnp.einsum('bhqk,bhkd->bhqd', p, v)

        def heads(x, nh, hd):
            b, l, _ = x.shape
            return x.reshape(b, l, nh, hd).transpose(0, 2, 1, 3)
        b, l, _ = hidden_states.shape
        vm = expert_mask(token_type_ids)[..., None]
        residual = hidden_states
        x = rms_norm(hidden_states, ln_in_w)
        mixed = jnp.where(vm, x @ v_qkv, x @ l_qkv)
        q, k, v = jnp.split(mixed, 3, axis=-1)
        q, k, v = (heads(q, NH, HD), heads(k, NH, HD), heads(v, NH, HD))
        q, k = apply_rotary(q, k, position_ids, l)
        ctx = sdpa(q, k, v, causal=True)
        ctx = ctx.transpose(0, 2, 1, 3).reshape(b, l, H)
        attn_out = jnp.where(vm, ctx @ v_dense, ctx @ l_dense)
        hidden_states = residual + attn_out
        ci = rms_norm(hidden_states, ln_post_cross_w)
        cq = heads(ci @ cq_w, NH, CHD)
        ckv = encoder_outputs @ ckv_w
        ck, cv = jnp.split(ckv, 2, axis=-1)
        ck, cv = (heads(ck, NH, CHD), heads(cv, NH, CHD))
        cctx = sdpa(cq, ck, cv, causal=False)
        cctx = cctx.transpose(0, 2, 1, 3).reshape(b, l, CC)
        hidden_states = hidden_states + cctx @ cdense_w
        mi = rms_norm(hidden_states, ln_post_attn_w)
        v_out = jax.nn.silu(mi @ v_gate) * (mi @ v_up) @ v_down
        l_out = jax.nn.silu(mi @ l_gate) * (mi @ l_up) @ l_down
        hidden_states = hidden_states + jnp.where(vm, v_out, l_out)
        return hidden_states

    def _L3_xattn_ref(hidden_states, memory, W_mem, W_gate, b_gate, norm_w):
        import jax, jax.numpy as jnp
        import numpy as np
        EPS = 1e-06

        def _rmsnorm(x, w):
            var = jnp.mean(jnp.square(x), axis=-1, keepdims=True)
            return x * jax.lax.rsqrt(var + EPS) * w
        D = hidden_states.shape[-1]
        memory_proj = jnp.einsum('bme,de->bmd', memory, W_mem)
        scores = jnp.einsum('bnd,bmd->bnm', hidden_states, memory_proj) / jnp.sqrt(jnp.float32(D))
        attn = jax.nn.softmax(scores, axis=-1)
        memory_context = jnp.einsum('bnm,bmd->bnd', attn, memory_proj)
        gate_input = jnp.concatenate([hidden_states, memory_context], axis=-1)
        gate = jax.nn.sigmoid(jnp.einsum('bnf,df->bnd', gate_input, W_gate) + b_gate)
        fused = hidden_states + gate * memory_context
        return _rmsnorm(fused, norm_w)
    x = _L0_xattn_ref(x, ctx_1024, mask_BxS2_bk0, L0_xattn_ln_q_g, L0_xattn_ln_q_b, L0_xattn_Wq, L0_xattn_Wkv, L0_xattn_Wo, L0_xattn_attn_gate, L0_xattn_ln_ff_g, L0_xattn_ln_ff_b, L0_xattn_W1, L0_xattn_W2, L0_xattn_ff_gate)
    x = _L1_xattn_ref(x, ctx_1024, L1_xattn_W_mem, L1_xattn_W_gate, L1_xattn_b_gate, L1_xattn_norm_w)
    x = _L2_xattn_ref(x, ctx_1024, mask_BxS_ik0, pos_1xS, L2_xattn_ln_in_w, L2_xattn_ln_post_attn_w, L2_xattn_ln_post_cross_w, L2_xattn_v_qkv, L2_xattn_l_qkv, L2_xattn_v_dense, L2_xattn_l_dense, L2_xattn_cq_w, L2_xattn_ckv_w, L2_xattn_cdense_w, L2_xattn_v_gate, L2_xattn_v_up, L2_xattn_v_down, L2_xattn_l_gate, L2_xattn_l_up, L2_xattn_l_down)
    x = _L3_xattn_ref(x, ctx_1024, L3_xattn_W_mem, L3_xattn_W_gate, L3_xattn_b_gate, L3_xattn_norm_w)
    return x

_drawn_inputs = setup_inputs


def setup_inputs(seed=0):
    import zlib

    import numpy as np

    out = dict(_drawn_inputs(seed))
    spreads = {'L0_xattn_ln_q_g': (1.0, 0.6),
     'L0_xattn_ln_q_b': (0.0, 0.8),
     'L0_xattn_ln_ff_g': (1.0, 0.6),
     'L0_xattn_ln_ff_b': (0.0, 0.8),
     'L1_xattn_norm_w': (1.0, 0.2),
     'L2_xattn_ln_in_w': (1.0, 0.6),
     'L2_xattn_ln_post_attn_w': (1.0, 0.6),
     'L2_xattn_ln_post_cross_w': (1.0, 0.6),
     'L3_xattn_norm_w': (1.0, 0.2)}
    factors = {'L0_xattn_W1': 2.725,
     'L1_xattn_b_gate': 25.74,
     'L2_xattn_v_qkv': 8.0,
     'L2_xattn_v_dense': 6.27,
     'L2_xattn_cq_w': 61.702,
     'L2_xattn_v_gate': 5.549,
     'L2_xattn_v_up': 5.557,
     'L2_xattn_v_down': 5.539,
     'L3_xattn_b_gate': 52.406,
     'L2_xattn_cdense_w': 2.668}
    for name, (base, spread) in spreads.items():
        noise = np.random.default_rng([zlib.crc32(name.encode()), seed]).standard_normal(out[name].shape)
        drawn = base * np.exp(spread * noise) if base else spread * noise
        out[name] = jnp.asarray(drawn.astype(out[name].dtype))
    for name, factor in factors.items():
        out[name] = (out[name] * factor).astype(out[name].dtype)
    return out
```

```python
from contextlib import ExitStack

import numpy as np

import concourse.bass as bass
from concourse import mybir

F32 = mybir.dt.float32
F32R = mybir.dt.float32r
I32 = mybir.dt.int32
U8 = mybir.dt.uint8
ACT = mybir.ActivationFunctionType
ALU = mybir.AluOpType
AX = mybir.AxisListType

P = 128
B, NT, D = 4, 256, 256
TT = NT // P
DC = D // P
S2, M = 1601, 128
KT = -(-S2 // P)
SK = KT * P
HALF, QUART = SK // 2, SK // 4
LAST = S2 - (KT - 1) * P
H0, HD0 = 16, 64
PAIRS = H0 // 2
FF = 1024
H2, HD2, HC2 = 16, 16, 8
FI, FIP = 688, 768
NEG = -1e30
CONSTS = 7

LNQ_G, LNQ_B, LNF_G, LNF_B, W_IN, W_CROSS, W_POST = range(0, 14, 2)

R_ID, R_TRIQ, R_TRIK, R_SHA, R_SHB = range(5)
R_SELF = 5
R_CROSS = R_SELF + 16
N_R = R_CROSS + 16
C_ID, C_ONES, C_SELS, C_SELC, C_COS, C_SIN = 0, 1, 2, 3, 4, 6
N_C = 8
(K_POS0, K_POS1, K_OH_A, K_OH_B, K_OH_SELF, K_OH_CROSS, K_PAD_CROSS, K_Q_CROSS, K_ROW96, K_SHQ) = range(10)
N_K = 10


def constants():
    r = np.zeros((N_R, P, P), np.float32)
    i = np.arange(P)
    r[R_ID] = np.eye(P)
    r[R_TRIQ] = np.where(i[None, :] <= i[:, None], 0.0, NEG)
    r[R_TRIK] = r[R_TRIQ].T
    r[R_SHA][0] = 1.0
    r[R_SHB][0] = 1.0
    r[R_SHB][32, LAST:] = NEG
    for j in range(4):
        for h in range(2):
            for d in range(HD2):
                src, row = 32 * j + HD2 * h + d, 64 * h
                r[R_SELF + 4 * j + 0][src, row + d] = 1
                r[R_SELF + 4 * j + 0][src, row + 40 + d] = 1
                r[R_SELF + 4 * j + 1][src, row + 16 + d] = 1
                r[R_SELF + 4 * j + 2][src, row + d] = 1
                r[R_SELF + 4 * j + 2][src, row + 16 + d] = 1
                r[R_SELF + 4 * j + 3][src, row + 40 + d] = 1
        for h in range(4):
            for d in range(HC2):
                src, row = 32 * j + HC2 * h + d, 32 * h + 5
                r[R_CROSS + 4 * j + 0][src, row + d] = 1
                r[R_CROSS + 4 * j + 0][src, row + 16 + d] = 1
                r[R_CROSS + 4 * j + 1][src, row + 8 + d] = 1
                r[R_CROSS + 4 * j + 2][src, row + d] = 1
                r[R_CROSS + 4 * j + 2][src, row + 8 + d] = 1
                r[R_CROSS + 4 * j + 3][src, row + 16 + d] = 1
    c = np.zeros((N_C, P, P), np.float32)
    c[C_ID] = np.eye(P)
    c[C_ONES] = 1.0
    for h in range(4):
        c[C_SELS][32 * h + HD2, 32 * h:32 * h + 32] = 1
        c[C_SELC][32 * h + HC2, 32 * h:32 * h + 32] = 1
    inv = (np.float32(1.0) / np.float32(10000.0) ** (np.arange(0, HD2, 2, dtype=np.float32) / np.float32(HD2))).astype(np.float32)
    f = np.outer(np.arange(NT, dtype=np.float32), inv).astype(np.float32)
    emb = np.concatenate([f, f], -1)
    sign = np.where(np.arange(HD2) < HD2 // 2, -1.0, 1.0)
    for k in range(2):
        c[C_COS + k] = np.tile(np.cos(emb)[k * P:(k + 1) * P], (1, P // HD2))
        c[C_SIN + k] = np.tile((np.sin(emb) * sign)[k * P:(k + 1) * P], (1, P // HD2))
    k = np.zeros((P, N_K), np.float32)
    k[:, K_POS0], k[:, K_POS1] = i, i + P
    k[64, K_OH_A] = 1
    k[65, K_OH_B] = 1
    k[32, K_OH_SELF] = k[97, K_OH_SELF] = 1
    for h in range(4):
        k[33 * h, K_OH_CROSS] = k[33 * h, K_PAD_CROSS] = 1
        k[32 * h + 4, K_PAD_CROSS] = NEG
        k[32 * h + 4, K_Q_CROSS] = 1
    k[96, K_ROW96] = 1
    k[32, K_SHQ] = 1
    return (np.ascontiguousarray(r.transpose(1, 0, 2)), np.ascontiguousarray(c.transpose(1, 0, 2)), k)


class Signal:

    def __init__(self, handle, per, primed):
        self.handle, self.per, self.primed = handle, per, int(primed)

    def at(self, turn, n=None):
        n = self.per if n is None else n
        assert n > 0 or self.primed
        return turn * self.per + (n + self.primed)


def program(nc, io):
    with ExitStack() as ctx:
        top = [nc.sbuf_base]

        def place(name, shape, dt, where):
            size = int(np.prod(shape[1:])) * (1 if dt == U8 else 4)
            off = -(-where[0] // 64) * 64
            where[0] = off + size
            return nc.alloc_sbuf_tensor_at(name, shape, dt, offset=off)

        def sb(name, shape, dt=F32):
            return place(name, shape, dt, top)

        def psum(name, cols):
            return ctx.enter_context(nc.psum_tensor(name, [P, cols], F32))

        def sig(name, per=1, primed=False):
            return Signal(ctx.enter_context(nc.semaphore(name)), per, primed)

        cr = sb("const_r", [P, N_R, P], F32R)
        cc = sb("const_f", [P, N_C, P])
        ck = sb("const_cols", [P, N_K])
        feat = sb("feature_scalars", [P, 14])
        gates = sb("gates", [P, 2])
        tgate = sb("tanh_gates", [P, 2])
        rows = sb("row_params", [P, 4, D])
        wm = sb("w_mem", [P, 2, DC, M])
        wmT = sb("w_mem_t", [P, 2, D])
        wg = sb("w_gate", [P, 2, 2 * DC, D])
        wo = sb("w_o", [P, PAIRS, D])
        cosT, sinT = sb("cos_t", [P, NT]), sb("sin_t", [P, NT])
        cth, ctl = sb("ctx_t_hi", [P, SK], F32R), sb("ctx_t_lo", [P, SK], F32R)
        ctxn = sb("ctx_rows", [P, KT, M])
        vmb = sb("expert_mask", [P, NT])
        valid = sb("batch_has_keys", [P, 2])
        gbf = sb("lnq_scaled", [P, 2 * DC])
        prob = sb("probs", [P, 4, 512])
        x0 = sb("x_in", [P, TT, D])
        xa, xb, xn = sb("x_a", [P, TT, D]), sb("x_b", [P, TT, D]), sb("x_normed", [P, TT, D])
        bn = sb("bn_stats", [P, TT, 6])
        mv = sb("mean_var", [P, TT, 2])
        rs = sb("rstd_work", [P, 5, TT])
        mxs = sb("max_parts", [P, 2, 4, 2])
        nmx = sb("neg_max", [P, 2, 4])
        rec = sb("recip_sum", [P, NT])
        acc = sb("prob_sums", [P, 2, 512])
        base = top[0]

        a = [base]
        par = []
        for s in range(2):
            par.append(dict(
                kst=place(f"k_hi_lo{s}", [P, 2, SK], F32R, a), kh1=place(f"k_hi_rows{s}", [P, 2, SK], F32R, a),
                v=place(f"v0_{s}", [P, KT, P], F32, a), qst=place(f"q_hi_hi{s}", [P, 2, NT], F32R, a),
                q2=place(f"q_lo_shift{s}", [P, 2, NT], F32R, a), qx=place(f"q_hi{s}", [P, 2, NT], F32R, a)))
        wraw = [place(f"w_pair{s}", [P, 4, P], F32, a) for s in range(2)]
        whi = [place(f"w_pair_hi{s}", [P, 4, P], F32R, a) for s in range(2)]
        wlo = [place(f"w_pair_lo{s}", [P, 4, P], F32R, a) for s in range(2)]
        xnt = place("xn_t", [P, DC, NT], F32, a)
        xnh, xnl = place("xn_t_hi", [P, DC, NT], F32R, a), place("xn_t_lo", [P, DC, NT], F32R, a)
        attn_at = a[0]
        attn = place("attn_t", [P, PAIRS, NT], F32, a)
        craw = place("ctx_t_raw", [P, SK], F32, [attn_at])
        mrow = prob[:].rearrange("p k n -> p (k n)")[:, 0:SK]
        craw_const = place("const_r_raw", [P, N_R, P], F32, [base])
        posi = place("positions_int", [P, NT], I32, [base + 20480])
        posf = place("positions", [P, NT], F32, [base + 21504])
        onehot = place("pos_onehot", [P, 2, NT], F32, [base + 22528])

        f = [base]
        w1 = place("w_ff1", [P, DC, FF], F32, f)
        w2 = place("w_ff2", [P, FF // P, D], F32, f)
        gt = place("gelu_t", [P, FF // P, NT], F32, f)
        ht = place("h_t", [P, DC, NT], F32, f)
        hst = place("hs_t", [P, DC, NT], F32, f)
        q1h, q1l = place("q1_hi", [P, NT], F32R, f), place("q1_lo", [P, NT], F32R, f)
        qs = place("q_shift", [P, NT], F32R, f)
        pct = place("pc_t", [P, NT], F32, f)
        mct, mc = place("mc_t", [P, DC, NT], F32, f), place("mc", [P, TT, D], F32, f)
        gz, gth = place("gate_in", [P, TT, D], F32, f), place("gate_tanh", [P, TT, D], F32, f)

        late_in = [f[0]]
        maskb, tids = place("mask_ints", [P, SK], I32, late_in), place("type_ids", [P, NT], I32, late_in)

        c = [base]
        xv, xl = place("x_v_t", [P, DC, NT], F32, c), place("x_l_t", [P, DC, NT], F32, c)
        xw = place("x_t", [P, DC, NT], F32, c)
        cx = place("ctx_heads_t", [P, 4, NT], F32, c)
        work_at = c[0]
        cxv, cxl = place("ctx_v_t", [P, 4, NT], F32, c), place("ctx_l_t", [P, 4, NT], F32, c)
        qn = place("qk_rot", [P, 2, NT], F32, c)
        qm = place("qk_sin", [P, 2, NT], F32, c)
        qkh = [place(f"qk_hi{m}", [P, 2, NT], F32R, c) for m in range(2)]
        qkl = [place(f"qk_lo{m}", [P, 2, NT], F32R, c) for m in range(2)]
        kp = [place(f"k_stack{s}", [P, NT], F32R, c) for s in range(3)]
        qb = [place(f"q_blocks{s}", [P, 2, NT], F32R, c) for s in range(3)]
        vs = place("v_self", [P, TT, H2, 32], F32, c)
        e = [work_at]
        cqh, cql = place("cq_hi", [P, NT], F32R, e), place("cq_lo", [P, NT], F32R, e)
        qb2 = [place(f"cq_blocks{s}", [P, 4, NT], F32R, e) for s in range(2)]
        knh, knl = place("ck_hi", [P, SK], F32R, e), place("ck_lo", [P, SK], F32R, e)
        ks2 = [place(f"ck_stack{s}", [P, SK], F32R, e) for s in range(2)]
        e = [max(c[0], e[0])]
        vx = place("v_cross", [P, KT, H2, 32], F32, e)
        g = [work_at]
        hv, hl = place("h_v", [P, 6, NT], F32, g), place("h_l", [P, 6, NT], F32, g)
        sg, hh = place("silu", [P, 2, NT], F32, g), place("hidden", [P, 2, NT], F32, g)
        w = [max(e[0], c[0], f[0])]
        wcq = place("w_cq", [P, DC, P], F32, w)
        wck = place("w_ckv", [P, 2, P], F32, w)
        wckh, wckl = place("w_ckv_hi", [P, 2, P], F32R, w), place("w_ckv_lo", [P, 2, P], F32R, w)
        wcd = place("w_cd", [P, 4, D], F32, w)
        late = w[0]
        wqk = place("w_qk", [P, 2, DC, 2, 4, P], F32, w)
        wv = place("w_v", [P, 2, DC, D], F32, w)
        wd = place("w_dense", [P, 2, 4, D], F32, w)
        z = [late]
        wgu = place("w_gate_up", [P, 2, DC, 2, FIP], F32, z)
        wdn = place("w_down", [P, 2, 6, D], F32, z)
        assert max(a[0], w[0], z[0]) <= nc.sbuf_usable_end

        X = [psum("x0", 1024), psum("x1", 1024)]
        ST = [psum("st0", 512), psum("st1", 512)]
        PV = psum("pv", 512)
        MI = psum("mi", 512)

        weights_in = sig("weights_in")
        const_in, const_r, const_t = sig("const_in"), sig("const_r", 3), sig("const_trig", 3)
        batch_in, rows_in, w_ff_in, w_l2_in, w_mlp_in = (sig(n, p) for n, p in (
            ("batch_in", 4 * 16), ("ctx_rows_in", 16), ("w_ff_in", 32), ("w_l2_in", 6 * 16), ("w_mlp_in", 32)))
        out_stored = sig("out_stored", 16, primed=True)
        cth_ready, ctl_ready, types_read = sig("ctx_hi_ready"), sig("ctx_lo_ready"), sig("types_read")
        batch_ready = sig("batch_ready")
        krows_ready = sig("krows_ready")
        chain = sig("dve_chain", 162)
        x_in, xt_mm, xt_read = sig("x_in", 7), sig("xt_mm", 7), sig("xt_read", 7)
        w_in, w_split = [sig(f"w_in{s}", 8) for s in range(2)], sig("w_split", 2)
        q_mm, q_hi, q_lo, q_dup = sig("q_mm"), sig("q_hi", 2, primed=True), sig("q_lo", primed=True), sig("q_dup")
        k_mm, k_hi, k_lo, k_one = sig("k_mm", 2), sig("k_hi", 4), sig("k_lo", 2), sig("k_one", 2)
        v_mm, v_read = sig("v_mm", 4), sig("v_read", 4)
        max_mm, max_read = sig("max_mm", 8), sig("max_read", 8, primed=True)
        nmax, nmax_t, shift_set = sig("nmax"), sig("nmax_t"), sig("shift_set")
        st_mm, p_exp, pv_mm = sig("st_mm", KT), sig("p_exp", KT, primed=True), sig("pv_mm", KT, primed=True)
        add_pool, add_dve = sig("add_pool", 6, primed=True), sig("add_dve", 5, primed=True)
        sum_mm, recip, norm = sig("sum_mm", primed=True), sig("recip"), sig("norm", primed=True)
        wo_mm, ff1_mm, gelu, ff2_mm = sig("wo_mm"), sig("ff1_mm", 2), sig("gelu", 2), sig("ff2_mm")
        q1_mm, q1_hi, q1_lo = sig("q1_mm"), sig("q1_hi"), sig("q1_lo")
        m1_mm, m1_read, nm1, nm1_t, q1_shift = sig("m1_mm", 4), sig("m1_read", 4, primed=True), sig("nm1"), sig("nm1_t"), sig("q1_shift")
        s1_mm, p1_exp, pv1_mm, add1 = sig("s1_mm", 7), sig("p1_exp", 7, primed=True), sig("pv1_mm", 7), sig("add1", 6)
        sum1_mm, pc_ready, mc_mm, mct_ready = sig("sum1_mm"), sig("pc_ready"), sig("mc_mm", 2), sig("mct_ready")
        gate_mm, gz_ready, gate_th = sig("gate_mm"), sig("gz_ready"), sig("gate_tanh_done")
        qk_mm, qk_read, v2_mm, v2_read = sig("qk_mm", 2), sig("qk_read", 2, primed=True), sig("v2_mm"), sig("v2_read")
        self_init = sig("self_init", 8)
        kq_mm, kq_read, blk_mm, ms_read = sig("kq_mm"), sig("kq_read", primed=True), sig("blk_mm"), sig("ms_read", primed=True)
        nms_t, ss_set, ss_mm, ps_exp, pvs_mm = sig("nms_t"), sig("ss_set", primed=True), sig("ss_mm", 2), sig("ps_exp", 2, primed=True), sig("pvs_mm", primed=True)
        cn_read, cn_sum = sig("cn_read", primed=True), sig("cn_sum", 2)
        cxm_ready, dense_mm = sig("cxm_ready"), sig("dense_mm")
        wck_split, ck_mm, ck_read, cv_mm, cv_read = sig("wck_split"), sig("ck_mm", 2), sig("ck_read", 2), sig("cv_mm", 4), sig("cv_read", 4)
        cross_init, cq_mm, cq_read = sig("cross_init", 2), sig("cq_mm"), sig("cq_read")
        ks_mm, ks_read, qg_mm, qg_read = sig("ks_mm", 2), sig("ks_read", 2), sig("qg_mm"), sig("qg_read", primed=True)
        mc2_mm, mc2_read, nmc, nmc_t, sc_set = sig("maxc_mm", 16), sig("maxc_read", 16, primed=True), sig("nmc"), sig("nmc_t"), sig("sc_set")
        sc_mm, pc_exp, pvc_mm = sig("sc_mm", 2 * KT), sig("pc_exp", 2 * KT, primed=True), sig("pvc_mm", 2 * KT, primed=True)
        cc_read, cc_sum, cc_ready, cd_mm = sig("cc_read", primed=True), sig("cc_sum", 2), sig("cc_ready"), sig("cd_mm")
        gu_mm, silu, hid, down_mm = sig("gu_mm"), sig("silu_done"), sig("hid"), sig("down_mm", primed=True)
        done = sig("batch_done", primed=True)
        passed = sig("wait_passed")

        def prime(eng, *signals):
            for s in signals:
                assert s.primed
                eng.sem_inc(s.handle, 1)

        def r32(ap):
            return ap.bitcast(F32)

        def ds(i, n=1):
            return bass.ds(i, n)

        def quads(eng, b, step):
            with eng.Fori(0, PAIRS // 2 - 1) as q:
                for s in range(2):
                    step(b, q * 2 + s, s, True, False)
            step(b, PAIRS - 2, 0, False, False)
            step(b, PAIRS - 1, 1, False, True)

        block = ctx.enter_context(nc.Block())

        @block.sync
        def _(sp):
            n = [0]

            def const(dst, src):
                sp.dma_start(dst, src).then_inc(const_in.handle, 16)
                n[0] += 16

            const(craw_const[:], io["const_r"])
            const(cc[:], io["const_f"])
            const(ck[:], io["const_k"])
            const(feat[:], io["feat"])
            const(gates[:], io["gates"].partition_broadcast(P))
            const(rows[:], io["rows"].partition_broadcast(P))
            const(posi[:], io["pos"].partition_broadcast(P))
            assert n[0] == CONSTS * 16
            with sp.Fori(0, B) as b:
                sp.wait_ge(down_mm.handle, down_mm.at(b, 0))
                sp.sem_inc(passed.handle, 1)
                sp.dma_start(maskb[:], io["mask"][ds(b)].rearrange("o s -> (o s)").partition_broadcast(P)).then_inc(batch_in.handle, 16)
                sp.dma_start(x0[:], io["x"][ds(b)].rearrange("o p t d -> (o p) t d")).then_inc(batch_in.handle, 16)
                sp.dma_start(craw[:], io["ctxT"][ds(b)].rearrange("o p s -> (o p) s")).then_inc(batch_in.handle, 16)
                sp.dma_start(tids[:], io["types"][ds(b)].rearrange("o s -> (o s)").partition_broadcast(P)).then_inc(batch_in.handle, 16)

                def load_pair(p, s):
                    sp.dma_start(wraw[s][:], io["w0"][ds(p)].rearrange("o p k n -> (o p) k n")).then_inc(w_in[s].handle, 16)

                load_pair(0, 0)
                load_pair(1, 1)
                sp.wait_ge(done.handle, done.at(b, 0))
                sp.sem_inc(passed.handle, 1)
                sp.dma_start(ctxn[:], io["ctxn"][ds(b)].rearrange("o p k m -> (o p) k m")).then_inc(rows_in.handle, 16)

                def step(b, p, s, more, last):
                    if more:
                        sp.wait_ge(w_split.handle, w_split.at(b * PAIRS + p, 2))
                        sp.sem_inc(passed.handle, 1)
                        load_pair(p + 2, s)
                quads(sp, b, step)
                sp.wait_ge(pv_mm.handle, pv_mm.at(b * PAIRS + PAIRS - 2))
                sp.sem_inc(passed.handle, 1)
                sp.dma_start(w1[:], io["w1"]).then_inc(w_ff_in.handle, 16)
                sp.dma_start(w2[:], io["w2"]).then_inc(w_ff_in.handle, 16)
                sp.wait_ge(norm.handle, norm.at(b * PAIRS + PAIRS - 1))
                sp.sem_inc(passed.handle, 1)
                sp.wait_ge(wo_mm.handle, wo_mm.at(b))
                sp.sem_inc(passed.handle, 1)
                for dst, name in ((wcq, "wcq"), (wck, "wckv"), (wcd, "wcd"), (wqk, "wqk"), (wv, "wv2"), (wd, "wd")):
                    sp.dma_start(dst[:], io[name]).then_inc(w_l2_in.handle, 16)
                sp.wait_ge(dense_mm.handle, dense_mm.at(b))
                sp.sem_inc(passed.handle, 1)
                sp.dma_start(wgu[:], io["wgu"]).then_inc(w_mlp_in.handle, 16)
                sp.dma_start(wdn[:], io["wdn"]).then_inc(w_mlp_in.handle, 16)

        @block.gpsimd
        def _(pool):
            prime(pool, add_pool)
            with pool.Fori(0, B) as b:
                pool.wait_ge(batch_ready.handle, batch_ready.at(b))
                pool.sem_inc(passed.handle, 1)
                for s in range(2):
                    t = par[s]
                    for h in range(2):
                        pool.tensor_scalar(t["kh1"][64:128, h, :], mrow[64:128, :], 1.0,
                                           ck[64:128, K_OH_A + h:K_OH_A + h + 1], ALU.mult, ALU.add)
                    for h in range(2):
                        for q in ("q2", "qx"):
                            m = pool.tensor_scalar(t[q][64:128, h, :], mrow[64:128, 0:NT], 0.0,
                                                   ck[64:128, K_ROW96:K_ROW96 + 1], ALU.mult, ALU.add)
                m.then_inc(krows_ready.handle, 1)

                def prep(i, s):
                    t = par[s]
                    pool.wait_ge(q_hi.handle, q_hi.at(i))
                    pool.sem_inc(passed.handle, 1)
                    pool.tensor_scalar(t["qst"][0:64], r32(t["qx"][0:64]), 1.0, 0.0, ALU.mult, ALU.add)
                    pool.tensor_scalar(t["qst"][64:128], r32(t["qx"][0:64]), 1.0, 0.0, ALU.mult, ALU.add)\
                        .then_inc(q_dup.handle, 1)
                    pool.wait_ge(q_dup.handle, q_dup.at(i))
                    for j in range(2):
                        pool.wait_ge(k_hi.handle, k_hi.at(i, 2 * j + 2))
                        pool.sem_inc(passed.handle, 1)
                        c = slice(j * HALF, (j + 1) * HALF)
                        pool.tensor_scalar(t["kh1"][0:64, :, c], r32(t["kst"][0:64, :, c]), 1.0, 0.0, ALU.mult, ALU.add)\
                            .then_inc(k_one.handle, 1)

                prep(b * PAIRS, 0)
                prep(b * PAIRS + 1, 1)

                def step(b, p, s, more, last):
                    i = b * PAIRS + p
                    for n in range(6):
                        if n == 0:
                            pool.wait_ge(p_exp.handle, p_exp.at(i, 3))
                            pool.wait_ge(sum_mm.handle, sum_mm.at(i, 0))
                            pool.tensor_tensor(acc[:, 0], prob[:, 0], prob[:, 2], ALU.add).then_inc(add_pool.handle, 1)
                        else:
                            pool.wait_ge(p_exp.handle, p_exp.at(i, 2 * n + 3))
                            pool.wait_ge(add_pool.handle, add_pool.at(i, n))
                            pool.tensor_tensor(acc[:, 0], acc[:, 0], prob[:, (2 * n + 2) % 4], ALU.add)\
                                .then_inc(add_pool.handle, 1)
                    if more:
                        pool.wait_ge(add_pool.handle, add_pool.at(i))
                        prep(i + 2, s)
                quads(pool, b, step)

                pool.wait_ge(gate_mm.handle, gate_mm.at(b * 2))
                pool.wait_ge(x_in.handle, x_in.at(b, 4))
                pool.sem_inc(passed.handle, 1)
                inits = [(vs[:], 0.0), (vs[:, :, :, HD2:HD2 + 1], 1.0)]
                for k in range(3):
                    inits += [(r32(qb[k][64:128, 0]), 0.0), (r32(qb[k][0:64, 1]), 0.0)]
                for s, steps in ((self_init, inits), (cross_init, [(vx[:], 0.0), (vx[:, :, :, HC2:HC2 + 1], 1.0)])):
                    for n, (dst, value) in enumerate(steps):
                        pool.memset(dst, value).then_inc(s.handle, 1)
                        pool.wait_ge(s.handle, s.at(b, n + 1))
                        pool.sem_inc(passed.handle, 1)

        @block.scalar
        def _(act):
            prime(act, out_stored, kq_read, q_hi, p_exp, p1_exp, ps_exp, pc_exp)
            act.wait_ge(const_in.handle, CONSTS * 16)
            for dst, name in ((wo, "wo"), (wm, "wm"), (wmT, "wmT"), (wg, "wg")):
                act.dma_start(dst[:], io[name]).then_inc(weights_in.handle, 16)
            act.activation(tgate[:], gates[:], ACT.Tanh).then_inc(const_r.handle, 1)
            with act.Fori(0, B) as b:
                def prep(i, s, p):
                    t = par[s]

                    def keys(j):
                        act.wait_ge(k_mm.handle, k_mm.at(i, j + 1))
                        for h in range(2):
                            act.activation(
                                t["kst"][0:64, h, j * HALF:(j + 1) * HALF].rearrange("p (c n) -> p c n", c=2),
                                X[j][64 * h:64 * h + 64, :].rearrange("p (c n) -> p c n", c=2)[:, :, 0:QUART],
                                ACT.Copy).then_inc(k_hi.handle, 1)

                    def values(j):
                        k0, k1 = 4 * j, min(4 * j + 4, KT)
                        act.wait_ge(v_mm.handle, v_mm.at(i, j + 1))
                        act.activation(t["v"][:, k0:k1].rearrange("p k n -> p (k n)"), ST[j % 2][:, 0:(k1 - k0) * P], ACT.Copy)\
                            .then_inc(v_read.handle, 1)

                    act.wait_ge(q_mm.handle, q_mm.at(i))
                    for h in range(2):
                        act.activation(t["qx"][0:64, h], MI[64 * h:64 * h + 64, 0:NT], ACT.Copy).then_inc(q_hi.handle, 1)
                    if p is None:
                        values(0)
                    keys(0)
                    keys(1)
                    for j in range(0 if p is not None else 1, 4):
                        values(j)

                act.wait_ge(batch_in.handle, batch_in.at(b))
                act.wait_ge(done.handle, done.at(b, 0))
                act.activation(cth[:], craw[:], ACT.Copy).then_inc(cth_ready.handle, 1)
                prep(b * PAIRS, 0, 0)
                act.wait_ge(types_read.handle, types_read.at(b))
                prep(b * PAIRS + 1, 1, 1)

                def step(b, p, s, more, last):
                    i = b * PAIRS + p
                    for kt in range(KT):
                        act.wait_ge(st_mm.handle, st_mm.at(i, kt + 1))
                        if kt < 4:
                            act.wait_ge(pv_mm.handle, pv_mm.at(i, 0))
                            act.wait_ge(add_pool.handle, add_pool.at(i, 0))
                            act.wait_ge(add_dve.handle, add_dve.at(i, 0))
                        else:
                            act.wait_ge(pv_mm.handle, pv_mm.at(i, kt - 3))
                            if kt % 2 == 0:
                                act.wait_ge(add_pool.handle, add_pool.at(i, max(1, (kt - 4) // 2)))
                            else:
                                act.wait_ge(add_dve.handle, add_dve.at(i, max(1, (kt - 5) // 2)))
                        act.activation(prob[:, kt % 4], ST[kt % 2][:], ACT.Exp, scale=HD0 ** -0.5).then_inc(p_exp.handle, 1)
                    if more:
                        prep(i + 2, s, None)
                quads(act, b, step)

                for j in range(2):
                    act.wait_ge(ff1_mm.handle, ff1_mm.at(b, j + 1))
                    act.activation(gt[:, 4 * j:4 * j + 4].rearrange("p k n -> p (k n)"), X[j][:], ACT.Gelu)\
                        .then_inc(gelu.handle, 1)

                def memory_layer(l):
                    i = b * 2 + l
                    act.wait_ge(q1_mm.handle, q1_mm.at(i))
                    act.activation(q1h[:], MI[:, 0:NT], ACT.Copy).then_inc(q1_hi.handle, 1)
                    for j in range(7):
                        n = 512 if j < 6 else NT
                        act.wait_ge(s1_mm.handle, s1_mm.at(i, j + 1))
                        if j >= 4:
                            act.wait_ge(pv1_mm.handle, pv1_mm.at(i, j - 3))
                            act.wait_ge(add1.handle, add1.at(i, max(1, j - 4)))
                        act.activation(prob[:, j % 4, 0:n], ST[j % 2][:, 0:n], ACT.Exp, scale=D ** -0.5)\
                            .then_inc(p1_exp.handle, 1)
                    act.wait_ge(mc_mm.handle, mc_mm.at(i, 1))
                    act.activation(mct[:].rearrange("p c n -> p (c n)"), X[0][:, 0:512], ACT.Copy).then_inc(mct_ready.handle, 1)
                    act.wait_ge(gz_ready.handle, gz_ready.at(i))
                    act.activation(gth[:], gz[:], ACT.Tanh, scale=0.5).then_inc(gate_th.handle, 1)

                memory_layer(0)

                act.wait_ge(v2_mm.handle, v2_mm.at(b))
                act.wait_ge(self_init.handle, self_init.at(b))
                act.activation(vs[:, :, :, 0:HD2], MI[:].rearrange("p (t h d) -> p t h d", t=TT, h=H2), ACT.Copy)\
                    .then_inc(v2_read.handle, 1)

                def stacks(j):
                    act.wait_ge(kq_mm.handle, kq_mm.at(b * 8 + j))
                    if j >= 3:
                        act.wait_ge(ss_mm.handle, ss_mm.at(b * 8 + j - 3))
                    act.activation(kp[j % 3][:], MI[:, 0:NT], ACT.Identity, bias=ck[:, K_OH_SELF:K_OH_SELF + 1])
                    for h in range(2):
                        r = slice(64 * h, 64 * h + 64)
                        m = act.activation(qb[j % 3][r, h], MI[r, NT:2 * NT], ACT.Copy)
                    m.then_inc(kq_read.handle, 1)

                stacks(0)
                stacks(1)
                for j in range(8):
                    i = b * 8 + j
                    if j < 6:
                        stacks(j + 2)
                    for u, n in enumerate((512, NT)):
                        act.wait_ge(ss_mm.handle, ss_mm.at(i, u + 1))
                        if j >= 2:
                            act.wait_ge(pvs_mm.handle, pvs_mm.at(i - 2))
                        act.activation(prob[:, 2 * (j % 2) + u, 0:n], ST[u][:, 0:n], ACT.Exp, scale=HD2 ** -0.5)\
                            .then_inc(ps_exp.handle, 1)

                act.wait_ge(cross_init.handle, cross_init.at(b))
                def keys(i, gr, j):
                    act.wait_ge(ks_mm.handle, ks_mm.at(i, j + 1))
                    if gr >= 2:
                        act.wait_ge(sc_mm.handle, sc_mm.at(i - 2))
                    dst, oh = ks2[gr % 2], ck[:, K_OH_CROSS:K_OH_CROSS + 1]
                    if j == 0:
                        m = act.activation(dst[:, 0:HALF].rearrange("p (c n) -> p c n", c=2),
                                           X[0][:].rearrange("p (c n) -> p c n", c=2)[:, :, 0:QUART], ACT.Identity, bias=oh)
                    else:
                        k0, k1 = HALF + QUART, S2 - HALF - QUART
                        act.activation(dst[:, HALF:k0], X[1][:, 0:QUART], ACT.Identity, bias=oh)
                        act.activation(dst[:, k0:S2], X[1][:, 512:512 + k1], ACT.Identity, bias=oh)
                        m = act.activation(dst[:, S2:SK], X[1][:, 512 + k1:512 + QUART], ACT.Identity,
                                           bias=ck[:, K_PAD_CROSS:K_PAD_CROSS + 1])
                    m.then_inc(ks_read.handle, 1)

                for j in range(2):
                    keys(b * 4, 0, j)
                for j in range(4):
                    act.wait_ge(cv_mm.handle, cv_mm.at(b, j + 1))
                    k0, k1 = 4 * j, min(4 * j + 4, KT)
                    act.activation(vx[:, k0:k1, :, 0:HC2],
                                   ST[j % 2][:, 0:(k1 - k0) * P].rearrange("p (k h d) -> p k h d", h=H2, d=HC2), ACT.Copy)\
                        .then_inc(cv_read.handle, 1)
                for gr in range(4):
                    i = b * 4 + gr
                    for kt in range(KT):
                        for u in range(2):
                            n = 2 * kt + u
                            act.wait_ge(sc_mm.handle, sc_mm.at(i, n + 1))
                            act.wait_ge(pvc_mm.handle, pvc_mm.at(i, max(0, n - 3)))
                            act.activation(prob[:, n % 4], ST[n % 2][:], ACT.Exp, scale=float(HC2) ** -0.5)\
                                .then_inc(pc_exp.handle, 1)
                        if gr < 3 and kt == 0:
                            keys(i + 1, gr + 1, 0)
                            keys(i + 1, gr + 1, 1)
                for m in range(6):
                    i = b * 6 + m
                    act.wait_ge(gu_mm.handle, gu_mm.at(i))
                    if m >= 2:
                        act.wait_ge(hid.handle, hid.at(i - 2))
                    act.activation(sg[:, m % 2], X[m % 2][:, 0:NT], ACT.Silu).then_inc(silu.handle, 1)

                memory_layer(1)
                act.wait_ge(done.handle, done.at(b, 1))
                act.dma_start(io["out"][ds(b)].rearrange("o p t d -> (o p) t d"), xb[:]).then_inc(out_stored.handle, 16)
            act.wait_ge(out_stored.handle, out_stored.at(B - 1))

        @block.tensor
        def _(pe):
            prime(pe, down_mm, sum_mm, pv_mm, pvs_mm, pvc_mm)
            def mm(out, lhsT, rhs, start=True, stop=True):
                return pe.matmul(out, lhsT, rhs, start=start, stop=stop, skip_group_check=True)

            ident, ones = cc[:, C_ID], cc[:, C_ONES]

            pe.wait_ge(const_in.handle, CONSTS * 16)
            pe.wait_ge(const_t.handle, const_t.at(0, 1))
            for k, tab in enumerate((C_COS, C_SIN)):
                for ch in range(2):
                    last = mm(MI[:, k * NT:(k + 1) * NT], cc[:, tab + ch], onehot[:, ch], ch == 0, ch == 1)
            last.then_inc(const_r.handle, 1)

            with pe.Fori(0, B) as b:
                def transposed(k, src):
                    pe.wait_ge(x_in.handle, x_in.at(b, k + 1))
                    for ch in range(DC):
                        for t in range(TT):
                            o = ch * NT + t * P
                            last = pe.transpose(X[0][:, o:o + P], src[:, t, ch * P:(ch + 1) * P], ident)
                    last.then_inc(xt_mm.handle, 1)

                transposed(0, xn)

                def prep_q(i, s, p):
                    pe.wait_ge(w_split.handle, w_split.at(i))
                    if p == 0:
                        pe.wait_ge(xt_read.handle, xt_read.at(b, 1))
                    if p != 0:
                        pe.wait_ge(q_lo.handle, q_lo.at(i, 0))
                        pe.wait_ge(q_hi.handle, q_hi.at(i, 0))
                    n = 0
                    for ch in range(DC):
                        for w, x in ((whi, xnh), (whi, xnl), (wlo, xnh)):
                            last = mm(MI[:, 0:NT], w[s][:, ch], x[:, ch], n == 0, n == 5)
                            n += 1
                    last.then_inc(q_mm.handle, 1)

                def prep_k(i, s, p):
                    if p == 0:
                        pe.wait_ge(ctl_ready.handle, ctl_ready.at(b))
                    for j in range(2):
                        if p == 1:
                            pe.wait_ge(k_lo.handle, k_lo.at(i - 1, j + 1))
                            pe.wait_ge(k_hi.handle, k_hi.at(i - 1, 2 * j + 2))
                        if p is None:
                            pe.wait_ge(max_read.handle, max_read.at(i - 1, 7 + j))
                        for n, (w, x) in enumerate(((whi, cth), (whi, ctl), (wlo, cth))):
                            for ch in range(2):
                                o = j * HALF + ch * QUART
                                last = mm(X[j][:, ch * 512:ch * 512 + QUART], w[s][:, 2], x[:, o:o + QUART], n == 0, n == 2)
                        last.then_inc(k_mm.handle, 1)

                def prep_v(i, s, j, p):
                    if j >= 2:
                        pe.wait_ge(v_read.handle, v_read.at(i, j - 1))
                    elif p == 1:
                        pe.wait_ge(v_read.handle, v_read.at(i - 1, 3 + j))
                    elif p is None and j == 1:
                        pe.wait_ge(shift_set.handle, shift_set.at(i - 1))
                    for kt in range(4 * j, min(4 * j + 4, KT)):
                        o = (kt % 4) * P
                        for n, (w, x) in enumerate(((whi, cth), (wlo, cth), (whi, ctl))):
                            last = mm(ST[j % 2][:, o:o + P], x[:, kt * P:(kt + 1) * P], w[s][:, 3], n == 0, n == 2)
                    last.then_inc(v_mm.handle, 1)

                def max_part(i, s, n):
                    t = par[s]
                    half, h, qt = n % 2, n // 2 % 2, n // 4
                    if n == 0:
                        pe.wait_ge(q_hi.handle, q_hi.at(i))
                        pe.wait_ge(k_one.handle, k_one.at(i))
                    if n < 2:
                        pe.wait_ge(k_lo.handle, k_lo.at(i, n + 1))
                        pe.wait_ge(k_hi.handle, k_hi.at(i, 2 * n + 2))
                        pe.wait_ge(max_read.handle, max_read.at(i, 0))
                    else:
                        pe.wait_ge(max_read.handle, max_read.at(i, n - 1))
                    for ch in range(2):
                        o = half * HALF + ch * QUART
                        last = mm(X[half][:, ch * 512:ch * 512 + QUART], t["qx"][:, h, qt * P:(qt + 1) * P],
                                  t["kh1"][:, h, o:o + QUART])
                    last.then_inc(max_mm.handle, 1)

                def shifts(i):
                    pe.wait_ge(nmax.handle, nmax.at(i))
                    for qt in range(TT):
                        tr = pe.transpose(ST[1][0:2, qt * P:(qt + 1) * P], nmx[:, qt, 0:2], ident)
                    tr.then_inc(nmax_t.handle, 1)

                i0 = b * PAIRS
                for p in range(2):
                    prep_q(i0 + p, p, p)
                    prep_k(i0 + p, p, p)
                    for j in range(4):
                        prep_v(i0 + p, p, j, p)
                pe.wait_ge(krows_ready.handle, krows_ready.at(b))
                pe.wait_ge(k_lo.handle, k_lo.at(i0 + 1))
                pe.wait_ge(k_hi.handle, k_hi.at(i0 + 1))
                for n in range(8):
                    max_part(i0, 0, n)
                pe.wait_ge(v_read.handle, v_read.at(i0 + 1))
                shifts(i0)

                def step(b, p, s, more, last_pair):
                    i = b * PAIRS + p
                    t = par[s]
                    def pv(kt):
                        pe.wait_ge(p_exp.handle, p_exp.at(i, kt + 1))
                        if kt == 0:
                            pe.wait_ge(norm.handle, norm.at(i, 0))
                            pe.wait_ge(v_read.handle, v_read.at(i))
                        for h in range(2):
                            r = slice(64 * h, 64 * h + 64)
                            m = mm(PV[r, 0:NT], t["v"][:, kt, r], prob[:, kt % 4, h * NT:(h + 1) * NT], kt == 0, kt == KT - 1)
                        m.then_inc(pv_mm.handle, 1)

                    for kt in range(KT):
                        if kt == 0:
                            pe.wait_ge(k_one.handle, k_one.at(i))
                            pe.wait_ge(k_lo.handle, k_lo.at(i))
                            pe.wait_ge(q_dup.handle, q_dup.at(i))
                            pe.wait_ge(q_lo.handle, q_lo.at(i))
                            pe.wait_ge(shift_set.handle, shift_set.at(i))
                            if not last_pair:
                                pe.wait_ge(v_read.handle, v_read.at(i + 1))
                        pe.wait_ge(p_exp.handle, p_exp.at(i, max(0, kt - 1)))
                        k = slice(kt * P, (kt + 1) * P)
                        for h in range(2):
                            o = ST[kt % 2][:, h * NT:(h + 1) * NT]
                            mm(o, t["kst"][:, h, k], t["qst"][:, h], True, False)
                            m = mm(o, t["kh1"][:, h, k], t["q2"][:, h], False, True)
                        m.then_inc(st_mm.handle, 1)
                        if not last_pair and 2 <= kt < 10:
                            max_part(i + 1, 1 - s, kt - 2)
                        if kt >= 2:
                            pv(kt - 2)
                    pv(KT - 2)
                    pv(KT - 1)
                    if not last_pair:
                        shifts(i + 1)
                    if more:
                        prep_q(i + 2, s, None)
                        prep_v(i + 2, s, 0, None)
                        prep_k(i + 2, s, None)
                    pe.wait_ge(add_pool.handle, add_pool.at(i))
                    pe.wait_ge(add_dve.handle, add_dve.at(i))
                    for h in range(2):
                        for k in range(2):
                            m = mm(PV[64 * h:64 * h + 64, NT:2 * NT], ones[:, 0:64], acc[:, k, h * NT:(h + 1) * NT], k == 0, k == 1)
                    m.then_inc(sum_mm.handle, 1)
                    if more:
                        for j in range(1, 4):
                            prep_v(i + 2, s, j, None)
                quads(pe, b, step)

                pe.wait_ge(weights_in.handle, 4 * 16)
                pe.wait_ge(norm.handle, norm.at(b * PAIRS + PAIRS - 1))
                for t in range(TT):
                    for p in range(PAIRS):
                        m = mm(X[0][:, t * D:(t + 1) * D], attn[:, p, t * P:(t + 1) * P], wo[:, p], p == 0, p == PAIRS - 1)
                m.then_inc(wo_mm.handle, 1)
                transposed(1, xn)
                pe.wait_ge(xt_read.handle, xt_read.at(b, 2))
                pe.wait_ge(w_ff_in.handle, w_ff_in.at(b))
                for j in range(2):
                    for k in range(4):
                        for ch in range(DC):
                            m = mm(X[j][:, k * NT:(k + 1) * NT], w1[:, ch, (4 * j + k) * P:(4 * j + k + 1) * P], ht[:, ch], ch == 0, ch == 1)
                    m.then_inc(ff1_mm.handle, 1)
                for t in range(TT):
                    for k in range(FF // P):
                        if t == 0 and k % 4 == 0:
                            pe.wait_ge(gelu.handle, gelu.at(b, k // 4 + 1))
                        m = mm(PV[:, t * D:(t + 1) * D], gt[:, k, t * P:(t + 1) * P], w2[:, k], k == 0, k == FF // P - 1)
                m.then_inc(ff2_mm.handle, 1)

                def memory_layer(l, src, k):
                    i = b * 2 + l
                    transposed(k, src)
                    pe.wait_ge(xt_read.handle, xt_read.at(b, k + 1))
                    for ch in range(DC):
                        m = mm(MI[:, 0:NT], wm[:, l, ch], hst[:, ch], ch == 0, ch == 1)
                    m.then_inc(q1_mm.handle, 1)
                    pe.wait_ge(q1_hi.handle, q1_hi.at(i))
                    for n in range(4):
                        qt, half = n // 2, n % 2
                        pe.wait_ge(m1_read.handle, m1_read.at(i, max(0, n - 1)))
                        for ch in range(2):
                            o = half * HALF + ch * QUART
                            w = QUART if n % 2 == 0 or ch == 0 else S2 + 1 - o
                            m = mm(X[half][:, ch * 512:ch * 512 + w], q1h[:, qt * P:(qt + 1) * P], cth[:, o:o + w])
                        m.then_inc(m1_mm.handle, 1)
                    pe.wait_ge(nm1.handle, nm1.at(i))
                    for qt in range(TT):
                        m = pe.transpose(MI[0:1, NT + qt * P:NT + (qt + 1) * P], nmx[:, qt, 0:1], ident)
                    m.then_inc(nm1_t.handle, 1)

                    if l == 0:
                        pe.wait_ge(rows_in.handle, rows_in.at(b))

                    def pv(j):
                        pe.wait_ge(p1_exp.handle, p1_exp.at(i, j + 1))
                        for kt in range(2 * j, min(2 * j + 2, KT)):
                            o = (kt % 2) * NT
                            m = mm(PV[:, 0:NT], ctxn[:, kt], prob[:, j % 4, o:o + NT], kt == 0, kt == KT - 1)
                        m.then_inc(pv1_mm.handle, 1)

                    for j in range(7):
                        pe.wait_ge(p1_exp.handle, p1_exp.at(i, max(0, j - 1)))
                        if j == 0:
                            pe.wait_ge(q1_lo.handle, q1_lo.at(i))
                            pe.wait_ge(q1_shift.handle, q1_shift.at(i))
                        for kt in range(2 * j, min(2 * j + 2, KT)):
                            o = ST[j % 2][:, (kt % 2) * NT:(kt % 2 + 1) * NT]
                            c = slice(kt * P, (kt + 1) * P)
                            mm(o, cth[:, c], q1h[:], True, False)
                            mm(o, cth[:, c], q1l[:], False, False)
                            mm(o, ctl[:, c], q1h[:], False, False)
                            m = mm(o, cr[:, R_SHB if kt == KT - 1 else R_SHA], qs[:], False, True)
                        m.then_inc(s1_mm.handle, 1)
                        if j:
                            pv(j - 1)
                    pv(6)
                    pe.wait_ge(add1.handle, add1.at(i))
                    for k2 in range(2):
                        m = mm(PV[:, NT:2 * NT], ones, acc[:, 0, k2 * NT:(k2 + 1) * NT], k2 == 0, k2 == 1)
                    m.then_inc(sum1_mm.handle, 1)
                    pe.wait_ge(pc_ready.handle, pc_ready.at(i))
                    for ch in range(DC):
                        m = mm(X[0][:, ch * NT:(ch + 1) * NT], wmT[:, l, ch * P:(ch + 1) * P], pct[:])
                    m.then_inc(mc_mm.handle, 1)
                    for t in range(TT):
                        m = mm(X[1][:, t * D:(t + 1) * D], pct[:, t * P:(t + 1) * P], wmT[:, l])
                    m.then_inc(mc_mm.handle, 1)
                    for t in range(TT):
                        for n in range(4):
                            if n == 2 and t == 0:
                                pe.wait_ge(mct_ready.handle, mct_ready.at(i))
                            lhsT = hst[:, n, t * P:(t + 1) * P] if n < 2 else mct[:, n - 2, t * P:(t + 1) * P]
                            m = mm(MI[:, t * D:(t + 1) * D], lhsT, wg[:, l, n], n == 0, n == 3)
                    m.then_inc(gate_mm.handle, 1)

                memory_layer(0, xa, 2)

                transposed(3, xn)
                pe.wait_ge(xt_read.handle, xt_read.at(b, 4))
                pe.wait_ge(w_l2_in.handle, w_l2_in.at(b))
                for m2 in range(2):
                    for k in range(4):
                        n = 0
                        for e2, x in enumerate((xv, xl)):
                            for ch in range(DC):
                                m = mm(X[m2][:, k * NT:(k + 1) * NT], wqk[:, e2, ch, m2, k], x[:, ch], n == 0, n == 3)
                                n += 1
                    m.then_inc(qk_mm.handle, 1)
                for t in range(TT):
                    n = 0
                    for e2, x in enumerate((xv, xl)):
                        for ch in range(DC):
                            m = mm(MI[:, t * D:(t + 1) * D], x[:, ch, t * P:(t + 1) * P], wv[:, e2, ch], n == 0, n == 3)
                            n += 1
                m.then_inc(v2_mm.handle, 1)
                pe.wait_ge(v2_read.handle, v2_read.at(b))

                def build(j):
                    m2, r = j // 4, R_SELF + 4 * (j % 4)
                    pe.wait_ge(qk_read.handle, qk_read.at(b, m2 + 1))
                    pe.wait_ge(kq_read.handle, kq_read.at(b * 8 + j, 0))
                    mm(MI[:, 0:NT], cr[:, r], qkh[m2][:, 1], True, False)
                    mm(MI[:, 0:NT], cr[:, r + 1], qkl[m2][:, 1], False, True)
                    mm(MI[:, NT:2 * NT], cr[:, r + 2], qkh[m2][:, 0], True, False)
                    mm(MI[:, NT:2 * NT], cr[:, r + 3], qkl[m2][:, 0], False, True).then_inc(kq_mm.handle, 1)

                def self_max(j):
                    pe.wait_ge(kq_read.handle, kq_read.at(b * 8 + j))
                    if j >= 2:
                        pe.wait_ge(ms_read.handle, ms_read.at(b * 8 + j - 2))
                    for h in range(2):
                        o, q, k = X[j % 2][:, 512 * h:512 * h + 3 * P], qb[j % 3][:, h], kp[j % 3]
                        mm(o[:, 0:P], q[:, 0:P], k[:, 0:P], True, False)
                        mm(o[:, 0:P], cr[:, R_ID], cr[:, R_TRIQ], False, True)
                        mm(o[:, P:3 * P], q[:, P:2 * P], k[:], True, False)
                        m = mm(o[:, 2 * P:3 * P], cr[:, R_ID], cr[:, R_TRIQ], False, True)
                    m.then_inc(blk_mm.handle, 1)

                def self_pv(j):
                    i, q = b * 8 + j, j // 2
                    if j % 2 == 0:
                        pe.wait_ge(cn_read.handle, cn_read.at(b * 4 + max(0, q - 1), 0))
                    pe.wait_ge(ps_exp.handle, ps_exp.at(i))
                    for h in range(2):
                        hd = 2 * j + h
                        o = PV[32 * (hd % 4):32 * (hd % 4) + 32, (q % 2) * NT:(q % 2 + 1) * NT]
                        mm(o, vs[:, 0, hd], prob[:, 2 * (j % 2), h * NT:(h + 1) * NT], True, False)
                        m = mm(o[:, P:NT], vs[:, 1, hd], prob[:, 2 * (j % 2) + 1, h * P:(h + 1) * P], False, True)
                    m.then_inc(pvs_mm.handle, 1)

                build(0)
                self_max(0)
                build(1)
                for j in range(8):
                    i = b * 8 + j
                    q, k = qb[j % 3], kp[j % 3]
                    pe.wait_ge(ms_read.handle, ms_read.at(i))
                    pe.wait_ge(ss_set.handle, ss_set.at(b * 8 + max(0, j - 1), 0))
                    for qt in range(TT):
                        o = 512 * qt + 3 * P
                        m = pe.transpose(X[j % 2][0:2, o:o + P], nmx[:, qt, 2 * (j % 2):2 * (j % 2) + 2], ident)
                    m.then_inc(nms_t.handle, 1)
                    if j < 6:
                        build(j + 2)
                    if j < 7:
                        self_max(j + 1)
                    pe.wait_ge(ss_set.handle, ss_set.at(i))
                    pe.wait_ge(ps_exp.handle, ps_exp.at(i, 0))
                    for h in range(2):
                        o = ST[0][:, h * NT:(h + 1) * NT]
                        mm(o, k[:, 0:P], q[:, h], True, False)
                        m = mm(o[:, 0:P], cr[:, R_ID], cr[:, R_TRIK], False, True)
                    m.then_inc(ss_mm.handle, 1)
                    for h in range(2):
                        o = ST[1][:, h * P:(h + 1) * P]
                        mm(o, k[:, P:2 * P], q[:, h, P:2 * P], True, False)
                        m = mm(o, cr[:, R_ID], cr[:, R_TRIK], False, True)
                    m.then_inc(ss_mm.handle, 1)
                    if j:
                        self_pv(j - 1)
                    if j == 6:
                        pe.wait_ge(kq_read.handle, kq_read.at(b * 8 + 7))
                        pe.wait_ge(cn_read.handle, cn_read.at(b * 4 + 1))
                        mm(MI[:, 0:512], cc[:, C_SELS], cx[:, 0:2].rearrange("p k n -> p (k n)")).then_inc(cn_sum.handle, 1)
                self_pv(7)
                pe.wait_ge(cn_read.handle, cn_read.at(b * 4 + 3))
                mm(X[0][:, 0:512], cc[:, C_SELS], cx[:, 2:4].rearrange("p k n -> p (k n)")).then_inc(cn_sum.handle, 1)
                pe.wait_ge(cxm_ready.handle, cxm_ready.at(b))
                for t in range(TT):
                    n = 0
                    for e2, x in enumerate((cxv, cxl)):
                        for k in range(4):
                            m = mm(X[0][:, t * D:(t + 1) * D], x[:, k, t * P:(t + 1) * P], wd[:, e2, k], n == 0, n == 7)
                            n += 1
                m.then_inc(dense_mm.handle, 1)

                transposed(4, xn)
                pe.wait_ge(xt_read.handle, xt_read.at(b, 5))
                for ch in range(DC):
                    m = mm(MI[:, 0:NT], wcq[:, ch], xw[:, ch], ch == 0, ch == 1)
                m.then_inc(cq_mm.handle, 1)
                pe.wait_ge(wck_split.handle, wck_split.at(b))
                for j in range(2):
                    for n, (w, x) in enumerate(((wckh, cth), (wckh, ctl), (wckl, cth))):
                        for ch in range(2):
                            o = j * HALF + ch * QUART
                            m = mm(X[j][:, ch * 512:ch * 512 + QUART], w[:, 0], x[:, o:o + QUART], n == 0, n == 2)
                    m.then_inc(ck_mm.handle, 1)

                def cross_v(j):
                    if j >= 2:
                        pe.wait_ge(cv_read.handle, cv_read.at(b, j - 1))
                    for kt in range(4 * j, min(4 * j + 4, KT)):
                        o = (kt % 4) * P
                        for n, (w, x) in enumerate(((wckh, cth), (wckl, cth), (wckh, ctl))):
                            m = mm(ST[j % 2][:, o:o + P], x[:, kt * P:(kt + 1) * P], w[:, 1], n == 0, n == 2)
                    m.then_inc(cv_mm.handle, 1)

                pe.wait_ge(cq_read.handle, cq_read.at(b))

                def cross_stacks(gr, j):
                    i, r = b * 4 + gr, R_CROSS + 4 * gr
                    if j == 0:
                        pe.wait_ge(qg_read.handle, qg_read.at(i, 0))
                        mm(MI[:, 0:NT], cr[:, r + 2], cqh[:], True, False)
                        mm(MI[:, 0:NT], cr[:, r + 3], cql[:], False, True).then_inc(qg_mm.handle, 1)
                    if gr == 0:
                        pe.wait_ge(ck_read.handle, ck_read.at(b, 1 + j))
                    else:
                        pe.wait_ge(mc2_read.handle, mc2_read.at(i - 1, 15 + j))
                    for n, x in enumerate((knh, knl)):
                        for ch in range(2):
                            o = j * HALF + ch * QUART
                            m = mm(X[j][:, ch * 512:ch * 512 + QUART], cr[:, r + n], x[:, o:o + QUART], n == 0, n == 1)
                    m.then_inc(ks_mm.handle, 1)

                def cross_max(gr, n):
                    i = b * 4 + gr
                    half, h, qt = n % 2, n // 2 % 4, n // 8
                    if n < 2:
                        pe.wait_ge(ks_read.handle, ks_read.at(i))
                        pe.wait_ge(qg_read.handle, qg_read.at(i))
                    pe.wait_ge(mc2_read.handle, mc2_read.at(i, max(0, n - 1)))
                    for ch in range(2):
                        o = half * HALF + ch * QUART
                        m = mm(X[half][:, ch * 512:ch * 512 + QUART], qb2[gr % 2][:, h, qt * P:(qt + 1) * P], ks2[gr % 2][:, o:o + QUART])
                    m.then_inc(mc2_mm.handle, 1)

                for j in range(2):
                    cross_stacks(0, j)
                def cross_shifts(gr):
                    pe.wait_ge(nmc.handle, nmc.at(b * 4 + gr))
                    for qt in range(TT):
                        m = pe.transpose(MI[0:4, NT + qt * P:NT + (qt + 1) * P], nmx[:, qt, :], ident)
                    m.then_inc(nmc_t.handle, 1)

                for n in range(16):
                    cross_max(0, n)
                    if n % 4 == 1:
                        cross_v(n // 4)
                cross_shifts(0)
                for gr in range(4):
                    i = b * 4 + gr
                    pe.wait_ge(sc_set.handle, sc_set.at(i))
                    if gr == 0:
                        pe.wait_ge(cv_read.handle, cv_read.at(b))

                    def pv(kt):
                        for u in range(2):
                            n = 2 * kt + u
                            pe.wait_ge(pc_exp.handle, pc_exp.at(i, n + 1))
                            if n == 0:
                                pe.wait_ge(cc_read.handle, cc_read.at(i, 0))
                            for h in range(2):
                                hd = 2 * u + h
                                m = mm(PV[32 * hd:32 * hd + 32, 0:NT], vx[:, kt, 4 * gr + hd],
                                       prob[:, n % 4, h * NT:(h + 1) * NT], kt == 0, kt == KT - 1)
                            m.then_inc(pvc_mm.handle, 1)

                    for kt in range(KT):
                        for u in range(2):
                            n = 2 * kt + u
                            pe.wait_ge(pc_exp.handle, pc_exp.at(i, max(0, n - 1)))
                            m = mm(ST[n % 2][:], ks2[gr % 2][:, kt * P:(kt + 1) * P],
                                   qb2[gr % 2][:, 2 * u:2 * u + 2].rearrange("p h n -> p (h n)"))
                            m.then_inc(sc_mm.handle, 1)
                        if gr < 3 and kt == 0:
                            cross_stacks(gr + 1, 0)
                            cross_stacks(gr + 1, 1)
                        if gr < 3 and 1 <= kt < KT - 1:
                            for n in range((kt - 1) * 16 // (KT - 2), kt * 16 // (KT - 2)):
                                cross_max(gr + 1, n)
                        if gr == 3 and kt == 1:
                            pe.wait_ge(cc_read.handle, cc_read.at(i - 1))
                            mm(X[0][:, 0:512], cc[:, C_SELC], cx[:, 0:2].rearrange("p k n -> p (k n)"))
                            mm(X[0][:, 512:512 + NT], cc[:, C_SELC], cx[:, 2]).then_inc(cc_sum.handle, 1)
                        if kt:
                            pv(kt - 1)
                    pv(KT - 1)
                    if gr < 3:
                        cross_shifts(gr + 1)
                pe.wait_ge(cc_read.handle, cc_read.at(b * 4 + 3))
                mm(X[1][:, 0:NT], cc[:, C_SELC], cx[:, 3]).then_inc(cc_sum.handle, 1)
                pe.wait_ge(cc_ready.handle, cc_ready.at(b))
                for t in range(TT):
                    for k in range(4):
                        m = mm(X[0][:, t * D:(t + 1) * D], cx[:, k, t * P:(t + 1) * P], wcd[:, k], k == 0, k == 3)
                m.then_inc(cd_mm.handle, 1)

                transposed(5, xn)
                pe.wait_ge(xt_read.handle, xt_read.at(b, 6))
                pe.wait_ge(w_mlp_in.handle, w_mlp_in.at(b))
                for k in range(6):
                    i = b * 6 + k
                    if k >= 2:
                        pe.wait_ge(hid.handle, hid.at(i - 2))
                    for gu in range(2):
                        n = 0
                        for e2, x in enumerate((xv, xl)):
                            for ch in range(DC):
                                m = mm(X[k % 2][:, gu * 512:gu * 512 + NT], wgu[:, e2, ch, gu, k * P:(k + 1) * P], x[:, ch], n == 0, n == 3)
                                n += 1
                    m.then_inc(gu_mm.handle, 1)
                pe.wait_ge(hid.handle, hid.at(b * 6 + 5))
                for t in range(TT):
                    n = 0
                    for e2, x in enumerate((hv, hl)):
                        for k in range(6):
                            m = mm(PV[:, t * D:(t + 1) * D], x[:, k, t * P:(t + 1) * P], wdn[:, e2, k], n == 0, n == 11)
                            n += 1
                m.then_inc(down_mm.handle, 1)

                memory_layer(1, xa, 6)

        @block.vector
        def _(dve):
            prime(dve, add_dve, q_lo, max_read, norm, m1_read, qk_read, ms_read, qg_read, ss_set, cn_read, mc2_read, cc_read, done)
            count = [0]
            turn = [0]

            def link(ins):
                ins.then_inc(chain.handle, 1)
                count[0] += 1
                dve.wait_ge(chain.handle, turn[0] * chain.per + count[0])

            def ts(out, x, s1, s2, op0=ALU.mult, op1=ALU.add):
                return dve.tensor_scalar(out, x, s1, s2, op0, op1)

            def tt(out, x, y, op):
                return dve.tensor_tensor(out, x, y, op)

            dve.wait_ge(const_in.handle, CONSTS * 16)
            C = sig("const_chain", 100)
            k = [0]

            def clink(ins):
                ins.then_inc(C.handle, 1)
                k[0] += 1
                dve.wait_ge(C.handle, k[0])

            clink(dve.tensor_copy(posf[:], posi[:]))
            clink(dve.tensor_scalar(vmb[:], posf[:], 0.0, float(NT), ALU.is_lt, ALU.mult))
            clink(tt(posf[:], posf[:], vmb[:], ALU.add))
            clink(ts(posf[:], posf[:], 0.0, float(NT - 1), ALU.max, ALU.min))
            for ch in range(2):
                m = ts(onehot[:, ch], posf[:], ck[:, K_POS0 + ch:K_POS0 + ch + 1], None, ALU.is_equal, ALU.bypass)
            m.then_inc(const_t.handle, 1)
            dve.tensor_copy(cr[:], craw_const[:]).then_inc(const_t.handle, 1)
            dve.wait_ge(const_r.handle, const_r.at(0, 2))
            dve.tensor_copy(cosT[:], MI[:, 0:NT])
            dve.tensor_copy(sinT[:], MI[:, NT:2 * NT]).then_inc(const_t.handle, 1)
            dve.wait_ge(const_t.handle, const_t.at(0, 3))

            with dve.Fori(0, B) as b:
                turn[0] = b

                def normed(x, eps, rms, k):
                    rstd(x, eps, rms)
                    for t in range(TT):
                        if rms:
                            m = dve.tensor_scalar(xn[:, t], x[:, t], rs[:, 2, t:t + 1], None, ALU.mult)
                        else:
                            m = dve.tensor_scalar(xn[:, t], x[:, t], mv[:, t, 0:1], rs[:, 2, t:t + 1], ALU.subtract, ALU.mult)
                    m.then_inc(x_in.handle, 1)

                def rstd(x, eps, rms):
                    v, half, y, w = rs[:, 0], rs[:, 1], rs[:, 2], rs[:, 3]
                    for t in range(TT):
                        m = dve.bn_stats(bn[:, t], x[:, t])
                    link(m)
                    dve.sem_inc(passed.handle, 1)
                    for t in range(TT):
                        m = dve.bn_aggr(mv[:, t], bn[:, t])
                    link(m)
                    if rms:
                        link(tt(v, mv[:, :, 0], mv[:, :, 0], ALU.mult))
                        link(dve.scalar_tensor_tensor(v, v, eps, mv[:, :, 1], ALU.add, ALU.add))
                    else:
                        link(ts(v, mv[:, :, 1], eps, None, ALU.add, ALU.bypass))
                    dve.tensor_scalar(half, v, -0.5, None, ALU.mult)
                    link(dve.tensor_scalar(w.bitcast(I32), v.bitcast(I32), 1, None, ALU.logical_shift_right))
                    link(dve.tensor_scalar(y.bitcast(I32), w.bitcast(I32), -1.0, 1597463007.0, ALU.mult, ALU.add))
                    for _ in range(3):
                        link(tt(w, y, y, ALU.mult))
                        link(tt(w, w, half, ALU.mult))
                        link(dve.scalar_tensor_tensor(y, w, 1.5, y, ALU.add, ALU.mult))

                dve.wait_ge(batch_in.handle, batch_in.at(b))
                link(dve.tensor_reduce(valid[:, 0:1], maskb[:], AX.X, ALU.max))
                dve.tensor_scalar(gbf[:], feat[:, LNQ_G:LNQ_G + 4], valid[:, 0:1], None, ALU.mult)
                link(dve.tensor_scalar(valid[:, 1:2], valid[:, 0:1], ck[:, K_ROW96:K_ROW96 + 1], -NEG, ALU.mult, ALU.mult))
                link(ts(mrow[64:128, :], maskb[64:128, :], -1.0, valid[64:128, 1:2], ALU.add, ALU.mult))
                dve.memset(mrow[96:97, S2:SK], NEG).then_inc(batch_ready.handle, 1)

                normed(x0, 1e-5, False, 0)
                dve.wait_ge(xt_mm.handle, xt_mm.at(b, 1))
                for ch in range(DC):
                    m = ts(xnt[:, ch], X[0][:, ch * NT:(ch + 1) * NT], gbf[:, ch:ch + 1], gbf[:, 2 + ch:3 + ch])
                link(m)
                link(dve.tensor_copy(xnh[:], xnt[:]))
                tt(xnl[:], xnt[:], r32(xnh[:]), ALU.subtract).then_inc(xt_read.handle, 1)

                def split(i, s):
                    dve.wait_ge(w_in[s].handle, w_in[s].at(i, 16 - 8 * s))
                    dve.tensor_copy(whi[s][:], wraw[s][:]).then_inc(w_split.handle, 1)
                    dve.wait_ge(w_split.handle, w_split.at(i, 1))
                    tt(wlo[s][:], wraw[s][:], r32(whi[s][:]), ALU.subtract).then_inc(w_split.handle, 1)

                def prep(i, s):
                    t = par[s]
                    dve.wait_ge(q_hi.handle, q_hi.at(i))
                    for h in range(2):
                        m = tt(t["q2"][0:64, h], MI[64 * h:64 * h + 64, 0:NT], r32(t["qx"][0:64, h]), ALU.subtract)
                    m.then_inc(q_lo.handle, 1)
                    for j in range(2):
                        dve.wait_ge(k_hi.handle, k_hi.at(i, 2 * j + 2))
                        for h in range(2):
                            c = slice(j * HALF, (j + 1) * HALF)
                            m = tt(t["kst"][64:128, h, c].rearrange("p (c n) -> p c n", c=2),
                                   X[j][64 * h:64 * h + 64, :].rearrange("p (c n) -> p c n", c=2)[:, :, 0:QUART],
                                   r32(t["kst"][0:64, h, c]).rearrange("p (c n) -> p c n", c=2), ALU.subtract)
                        m.then_inc(k_lo.handle, 1)

                def max_part(i, n):
                    half, h, qt = n % 2, n // 2 % 2, n // 4
                    dve.wait_ge(max_mm.handle, max_mm.at(i, n + 1))
                    dve.tensor_reduce(mxs[:, qt, h, half:half + 1], X[half][:].rearrange("p (c n) -> p c n", c=2)[:, :, 0:QUART],
                                      AX.XY, ALU.max).then_inc(max_read.handle, 1)

                def neg_max(i):
                    dve.wait_ge(max_read.handle, max_read.at(i))
                    dve.tensor_reduce(nmx[:, :, 0:2], mxs[:, :, 0:2, :], AX.X, ALU.max, negate=True).then_inc(nmax.handle, 1)

                def shifts(i, s):
                    dve.wait_ge(nmax_t.handle, nmax_t.at(i))
                    dve.tensor_copy(par[s]["q2"][64:66], ST[1][0:2, 0:NT].rearrange("p (o n) -> p o n", o=1).to_broadcast([2, 2, NT]))\
                        .then_inc(shift_set.handle, 1)

                i0 = b * PAIRS
                split(i0, 0)
                dve.wait_ge(cth_ready.handle, cth_ready.at(b))
                tt(ctl[:], craw[:], r32(cth[:]), ALU.subtract).then_inc(ctl_ready.handle, 1)
                split(i0 + 1, 1)
                link(ts(rec[:], tids[:], 1.0, None, ALU.is_equal, ALU.bypass))
                dve.memset(vmb[:, NT - 1:NT], 0.0)
                tt(vmb[:, 0:NT - 1], rec[:, 0:NT - 1], rec[:, 1:NT], ALU.mult).then_inc(types_read.handle, 1)
                prep(i0, 0)
                prep(i0 + 1, 1)
                for n in range(8):
                    max_part(i0, n)
                neg_max(i0)
                shifts(i0, 0)

                def step(b, p, s, more, last_pair):
                    i = b * PAIRS + p
                    t = par[s]
                    if more:
                        dve.wait_ge(v_mm.handle, v_mm.at(i))
                        split(i + 2, s)
                    for kt in range(KT):
                        if kt % 2 and kt > 1:
                            n = (kt - 3) // 2
                            dve.wait_ge(p_exp.handle, p_exp.at(i, kt + 1))
                            if n == 0:
                                dve.wait_ge(sum_mm.handle, sum_mm.at(i, 0))
                                tt(acc[:, 1], prob[:, 1], prob[:, 3], ALU.add).then_inc(add_dve.handle, 1)
                            else:
                                dve.wait_ge(add_dve.handle, add_dve.at(i, n))
                                tt(acc[:, 1], acc[:, 1], prob[:, kt % 4], ALU.add).then_inc(add_dve.handle, 1)
                        if not last_pair and 2 <= kt < 10:
                            max_part(i + 1, kt - 2)
                    if not last_pair:
                        neg_max(i + 1)
                        shifts(i + 1, 1 - s)
                    if more:
                        prep(i + 2, s)
                    dve.wait_ge(sum_mm.handle, sum_mm.at(i))
                    dve.reciprocal(rec[:], PV[:, NT:2 * NT]).then_inc(recip.handle, 1)
                    dve.wait_ge(recip.handle, recip.at(i))
                    tt(attn[:, ds(p)].rearrange("p o n -> p (o n)"), PV[:, 0:NT], rec[:], ALU.mult).then_inc(norm.handle, 1)
                quads(dve, b, step)

                dve.wait_ge(wo_mm.handle, wo_mm.at(b))
                dve.wait_ge(out_stored.handle, out_stored.at(b, 0))
                link(dve.scalar_tensor_tensor(xb[:].rearrange("p t d -> p (t d)"), X[0][:, 0:512], tgate[:, 0:1],
                                              x0[:].rearrange("p t d -> p (t d)"), ALU.mult, ALU.add))
                normed(xb, 1e-5, False, 1)
                dve.wait_ge(xt_mm.handle, xt_mm.at(b, 2))
                for ch in range(DC):
                    m = ts(ht[:, ch], X[0][:, ch * NT:(ch + 1) * NT], feat[:, LNF_G + ch:LNF_G + ch + 1], feat[:, LNF_B + ch:LNF_B + ch + 1])
                m.then_inc(xt_read.handle, 1)
                dve.wait_ge(ff2_mm.handle, ff2_mm.at(b))
                dve.scalar_tensor_tensor(xa[:].rearrange("p t d -> p (t d)"), PV[:], tgate[:, 1:2],
                                         xb[:].rearrange("p t d -> p (t d)"), ALU.mult, ALU.add).then_inc(x_in.handle, 1)

                def memory_layer(l, k):
                    i = b * 2 + l
                    ts(qs[:], r32(cth[:, 0:NT]), 0.0, ck[:, K_SHQ:K_SHQ + 1])
                    dve.wait_ge(xt_mm.handle, xt_mm.at(b, k + 1))
                    dve.tensor_copy(hst[:].rearrange("p c n -> p (c n)"), X[0][:, 0:512]).then_inc(xt_read.handle, 1)
                    dve.wait_ge(q1_hi.handle, q1_hi.at(i))
                    tt(q1l[:], MI[:, 0:NT], r32(q1h[:]), ALU.subtract).then_inc(q1_lo.handle, 1)
                    for n in range(4):
                        qt, half = n // 2, n % 2
                        dve.wait_ge(m1_mm.handle, m1_mm.at(i, n + 1))
                        if half == 0:
                            m = dve.tensor_reduce(mxs[:, qt, 0, 0:1], X[0][:].rearrange("p (c n) -> p c n", c=2)[:, :, 0:QUART], AX.XY, ALU.max)
                        else:
                            dve.tensor_reduce(mxs[:, qt, 0, 1:2], X[1][:, 0:QUART], AX.X, ALU.max)
                            m = dve.tensor_reduce(mxs[:, qt, 1, 0:1], X[1][:, 512:512 + S2 - HALF - QUART], AX.X, ALU.max)
                        m.then_inc(m1_read.handle, 1)
                    dve.wait_ge(m1_read.handle, m1_read.at(i))
                    dve.tensor_reduce(nmx[:, :, 0:1], mxs[:].rearrange("p q k x -> p q (k x)")[:, :, 0:3], AX.X, ALU.max, negate=True)\
                        .then_inc(nm1.handle, 1)
                    dve.wait_ge(nm1_t.handle, nm1_t.at(i))
                    dve.tensor_copy(qs[0:1, :], MI[0:1, NT:2 * NT]).then_inc(q1_shift.handle, 1)
                    for j in range(1, 7):
                        dve.wait_ge(p1_exp.handle, p1_exp.at(i, j + 1))
                        if j == 1:
                            m = tt(acc[:, 0], prob[:, 0], prob[:, 1], ALU.add)
                        else:
                            dve.wait_ge(add1.handle, add1.at(i, j - 1))
                            n = 512 if j < 6 else NT
                            m = tt(acc[:, 0, 0:n], acc[:, 0, 0:n], prob[:, j % 4, 0:n], ALU.add)
                        m.then_inc(add1.handle, 1)
                    dve.wait_ge(sum1_mm.handle, sum1_mm.at(i))
                    link(dve.reciprocal(rec[:], PV[:, NT:2 * NT]))
                    tt(pct[:], PV[:, 0:NT], rec[:], ALU.mult).then_inc(pc_ready.handle, 1)
                    dve.wait_ge(mc_mm.handle, mc_mm.at(i))
                    link(dve.tensor_copy(mc[:].rearrange("p t d -> p (t d)"), X[1][:, 0:512]))
                    dve.wait_ge(gate_mm.handle, gate_mm.at(i))
                    tt(gz[:], MI[:].rearrange("p (t d) -> p t d", t=TT), rows[:, 2 + l:3 + l].to_broadcast([P, TT, D]), ALU.add)\
                        .then_inc(gz_ready.handle, 1)
                    dve.wait_ge(gate_th.handle, gate_th.at(i))
                    link(dve.scalar_tensor_tensor(gz[:], gth[:], 1.0, mc[:], ALU.add, ALU.mult))
                    link(dve.scalar_tensor_tensor(gth[:], gz[:], 0.5, xa[:], ALU.mult, ALU.add))
                    rstd(gth, 1e-6, True)
                    for t in range(TT):
                        m = dve.scalar_tensor_tensor(xb[:, t], gth[:, t], rs[:, 2, t:t + 1], rows[:, l], ALU.mult, ALU.mult)
                    if l == 1:
                        m.then_inc(done.handle, 1)
                    else:
                        link(m)

                memory_layer(0, 2)

                def scaled(k, w):
                    dve.wait_ge(xt_mm.handle, xt_mm.at(b, k + 1))
                    for ch in range(DC):
                        m = dve.tensor_scalar(xw[:, ch], X[0][:, ch * NT:(ch + 1) * NT], feat[:, w + ch:w + ch + 1], None, ALU.mult)
                    return m

                def by_expert(x, xe, xo, n):
                    mask = vmb[:].rearrange("p (o n) -> p o n", o=1).to_broadcast([P, n, NT])
                    link(tt(xe, x, mask, ALU.mult))
                    return tt(xo, x, xe, ALU.subtract)

                normed(xb, 1e-6, True, 3)
                link(scaled(3, W_IN))
                by_expert(xw[:], xv[:], xl[:], DC).then_inc(xt_read.handle, 1)
                for m2 in range(2):
                    dve.wait_ge(qk_mm.handle, qk_mm.at(b, m2 + 1))
                    dve.wait_ge(qk_read.handle, qk_read.at(b, m2))
                    x = X[m2][:].rearrange("p (k r n) -> p k r n", k=2, r=2)
                    tab = [w[:].rearrange("p (o n) -> p o n", o=1).to_broadcast([P, 2, NT]) for w in (cosT, sinT)]
                    tt(qn[:], x[:, :, 0], tab[0], ALU.mult)
                    link(tt(qm[:], x[:, :, 1], tab[1], ALU.mult))
                    link(tt(qn[:], qn[:], qm[:], ALU.add))
                    link(dve.tensor_copy(qkh[m2][:], qn[:]))
                    tt(qkl[m2][:], qn[:], r32(qkh[m2][:]), ALU.subtract).then_inc(qk_read.handle, 1)
                dve.wait_ge(self_init.handle, self_init.at(b))

                def self_max(j):
                    dve.wait_ge(blk_mm.handle, blk_mm.at(b * 8 + j))
                    for h in range(2):
                        x = X[j % 2][:, 512 * h:512 * h + 3 * P]
                        dve.tensor_reduce(mxs[:, 0, h, 0:1], x[:, 0:P], AX.X, ALU.max)
                        m = dve.tensor_reduce(mxs[:, 1, h, 0:1], x[:, P:3 * P], AX.X, ALU.max)
                    link(m)
                    o = 2 * (j % 2)
                    dve.tensor_scalar(nmx[:, :, o:o + 2], mxs[:, :, 0:2, 0], -1.0, None, ALU.mult).then_inc(ms_read.handle, 1)

                self_max(0)
                for j in range(8):
                    i = b * 8 + j
                    dve.wait_ge(nms_t.handle, nms_t.at(i))
                    shifts = X[j % 2][0:2].rearrange("p (c n) -> p c n", c=2)[:, :, 3 * P:4 * P]
                    for h in range(2):
                        m = dve.tensor_copy(qb[j % 3][64 * h + 32:64 * h + 34, h].rearrange("p (c n) -> p c n", c=2), shifts)
                    m.then_inc(ss_set.handle, 1)
                    if j < 7:
                        dve.wait_ge(ms_read.handle, ms_read.at(i))
                        self_max(j + 1)
                    if j and j % 2 == 0:
                        dve.wait_ge(pvs_mm.handle, pvs_mm.at(i - 1))
                        dve.tensor_copy(cx[:, j // 2 - 1], PV[:, (j // 2 - 1) % 2 * NT:((j // 2 - 1) % 2 + 1) * NT]).then_inc(cn_read.handle, 1)
                scratch = acc[:].rearrange("p k n -> p (k n)")

                def over_sums(k0, k1, sums):
                    part, c = scratch[:, k0 * NT:k1 * NT], cx[:, k0:k1].rearrange("p k n -> p (k n)")
                    link(dve.reciprocal(part, sums))
                    return tt(c, c, part, ALU.mult)

                dve.wait_ge(cn_sum.handle, cn_sum.at(b, 1))
                over_sums(0, 2, MI[:])
                dve.wait_ge(pvs_mm.handle, pvs_mm.at(b * 8 + 7))
                dve.tensor_copy(cx[:, 3], PV[:, NT:2 * NT]).then_inc(cn_read.handle, 1)
                dve.wait_ge(cn_sum.handle, cn_sum.at(b, 2))
                link(over_sums(2, 4, X[0][:, 0:512]))
                by_expert(cx[:], cxv[:], cxl[:], 4).then_inc(cxm_ready.handle, 1)
                dve.wait_ge(dense_mm.handle, dense_mm.at(b))
                link(tt(xa[:].rearrange("p t d -> p (t d)"), X[0][:, 0:512], xb[:].rearrange("p t d -> p (t d)"), ALU.add))

                normed(xa, 1e-6, True, 4)
                scaled(4, W_CROSS).then_inc(xt_read.handle, 1)
                dve.wait_ge(w_l2_in.handle, w_l2_in.at(b))
                link(dve.tensor_copy(wckh[:], wck[:]))
                tt(wckl[:], wck[:], r32(wckh[:]), ALU.subtract).then_inc(wck_split.handle, 1)
                dve.wait_ge(cq_mm.handle, cq_mm.at(b))
                link(dve.tensor_copy(cqh[:], MI[:, 0:NT]))
                tt(cql[:], MI[:, 0:NT], r32(cqh[:]), ALU.subtract).then_inc(cq_read.handle, 1)
                for j in range(2):
                    dve.wait_ge(ck_mm.handle, ck_mm.at(b, j + 1))
                    c = slice(j * HALF, (j + 1) * HALF)
                    x = X[j][:].rearrange("p (c n) -> p c n", c=2)[:, :, 0:QUART]
                    link(dve.tensor_copy(knh[:, c].rearrange("p (c n) -> p c n", c=2), x))
                    tt(knl[:, c].rearrange("p (c n) -> p c n", c=2), x,
                       r32(knh[:, c]).rearrange("p (c n) -> p c n", c=2), ALU.subtract).then_inc(ck_read.handle, 1)
                for k in range(2):
                    m = dve.memset(r32(qb2[k][:]), 0.0)
                link(m)

                def queries(gr):
                    i = b * 4 + gr
                    dve.wait_ge(qg_mm.handle, qg_mm.at(i))
                    if gr >= 2:
                        dve.wait_ge(sc_mm.handle, sc_mm.at(i - 2))
                    for h in range(4):
                        r = slice(32 * h, 32 * h + 32)
                        m = ts(qb2[gr % 2][r, h], MI[r, 0:NT], ck[r, K_Q_CROSS:K_Q_CROSS + 1], None, ALU.add, ALU.bypass)
                    m.then_inc(qg_read.handle, 1)

                def cross_max(gr):
                    for n in range(16):
                        half, h, qt = n % 2, n // 2 % 4, n // 8
                        dve.wait_ge(mc2_mm.handle, mc2_mm.at(b * 4 + gr, n + 1))
                        dve.tensor_reduce(mxs[:, qt, h, half:half + 1], X[half][:].rearrange("p (c n) -> p c n", c=2)[:, :, 0:QUART],
                                          AX.XY, ALU.max).then_inc(mc2_read.handle, 1)
                    dve.wait_ge(mc2_read.handle, mc2_read.at(b * 4 + gr))
                    dve.tensor_reduce(nmx[:], mxs[:], AX.X, ALU.max, negate=True).then_inc(nmc.handle, 1)

                def cross_shifts(gr):
                    dve.wait_ge(nmc_t.handle, nmc_t.at(b * 4 + gr))
                    for h in range(4):
                        m = dve.tensor_copy(qb2[gr % 2][32 * h:32 * h + 4, h], MI[0:4, NT:2 * NT])
                    m.then_inc(sc_set.handle, 1)

                queries(0)
                cross_max(0)
                cross_shifts(0)
                for gr in range(4):
                    i = b * 4 + gr
                    if gr < 3:
                        queries(gr + 1)
                        cross_max(gr + 1)
                        cross_shifts(gr + 1)
                    if gr == 3:
                        dve.wait_ge(cc_sum.handle, cc_sum.at(b, 1))
                        over_sums(0, 3, X[0][:, 0:3 * NT])
                    dve.wait_ge(pvc_mm.handle, pvc_mm.at(i))
                    dve.tensor_copy(cx[:, gr], PV[:, 0:NT]).then_inc(cc_read.handle, 1)
                dve.wait_ge(cc_sum.handle, cc_sum.at(b, 2))
                over_sums(3, 4, X[1][:, 0:NT]).then_inc(cc_ready.handle, 1)
                dve.wait_ge(cd_mm.handle, cd_mm.at(b))
                link(tt(xb[:].rearrange("p t d -> p (t d)"), X[0][:, 0:512], xa[:].rearrange("p t d -> p (t d)"), ALU.add))

                normed(xb, 1e-6, True, 5)
                link(scaled(5, W_POST))
                by_expert(xw[:], xv[:], xl[:], DC).then_inc(xt_read.handle, 1)
                for k in range(6):
                    i = b * 6 + k
                    dve.wait_ge(silu.handle, silu.at(i))
                    link(tt(hh[:, k % 2], sg[:, k % 2], X[k % 2][:, 512:512 + NT], ALU.mult))
                    link(tt(hv[:, k], hh[:, k % 2], vmb[:], ALU.mult))
                    tt(hl[:, k], hh[:, k % 2], hv[:, k], ALU.subtract).then_inc(hid.handle, 1)
                dve.wait_ge(down_mm.handle, down_mm.at(b))
                tt(xa[:].rearrange("p t d -> p (t d)"), PV[:], xb[:].rearrange("p t d -> p (t d)"), ALU.add).then_inc(x_in.handle, 1)

                memory_layer(1, 6)
            assert count[0] == chain.per, count[0]


_CONST = ("const_r", "const_f", "const_k")


def layouts(v):
    f = lambda name: np.asarray(v[name])

    def chunks(w):
        return w.reshape(-1, P, w.shape[1]).transpose(1, 0, 2)

    o = {}
    o["x"] = f("x").reshape(B, TT, P, D).transpose(0, 2, 1, 3)
    ctx = np.zeros((B, SK, M), np.float32)
    ctx[:, :S2] = f("ctx_1024")
    o["ctxT"] = ctx.transpose(0, 2, 1)
    o["ctxn"] = ctx.reshape(B, KT, P, M).transpose(0, 2, 1, 3)
    mask = np.zeros((B, SK), np.int32)
    mask[:, :S2] = f("mask_BxS2_bk0")
    o["mask"] = mask
    o["types"] = f("mask_BxS_ik0").astype(np.int32)
    o["pos"] = f("pos_1xS").astype(np.int32).reshape(NT)
    wq, wkv = f("L0_xattn_Wq"), f("L0_xattn_Wkv")
    w0 = np.zeros((PAIRS, P, 4, P), np.float32)
    for p in range(PAIRS):
        c = slice(p * P, (p + 1) * P)
        w0[p, :, 0], w0[p, :, 1] = wq[:P, c], wq[P:, c]
        w0[p, :, 2] = wkv[:, c]
        w0[p, :, 3] = wkv[:, H0 * HD0:][:, c]
    o["w0"] = w0
    o["wo"] = chunks(f("L0_xattn_Wo"))
    o["w1"] = chunks(f("L0_xattn_W1"))
    o["w2"] = chunks(f("L0_xattn_W2"))
    names = ("L0_xattn_ln_q_g", "L0_xattn_ln_q_b", "L0_xattn_ln_ff_g", "L0_xattn_ln_ff_b",
             "L2_xattn_ln_in_w", "L2_xattn_ln_post_cross_w", "L2_xattn_ln_post_attn_w")
    o["feat"] = np.concatenate([f(n).reshape(DC, P).T for n in names], 1)
    o["gates"] = np.concatenate([f("L0_xattn_attn_gate"), f("L0_xattn_ff_gate")])
    o["rows"] = np.stack([f("L1_xattn_norm_w"), f("L3_xattn_norm_w"), f("L1_xattn_b_gate"), f("L3_xattn_b_gate")])
    o["wm"] = np.stack([chunks(f(f"L{l}_xattn_W_mem")) for l in (1, 3)], 1)
    o["wmT"] = np.stack([f(f"L{l}_xattn_W_mem").T for l in (1, 3)], 1)
    o["wg"] = np.stack([chunks(f(f"L{l}_xattn_W_gate").T) for l in (1, 3)], 1)
    hd = np.arange(D).reshape(H2, 2, HD2 // 2)[:, ::-1].reshape(D)
    wqk = np.zeros((P, 2, DC, 2, 4, P), np.float32)
    wv = np.zeros((P, 2, DC, D), np.float32)
    wd = np.zeros((P, 2, 4, D), np.float32)
    wgu = np.zeros((P, 2, DC, 2, FIP), np.float32)
    wdn = np.zeros((2, FIP, D), np.float32)
    for e, x in enumerate("vl"):
        qkv = f(f"L2_xattn_{x}_qkv")
        for k, w in enumerate((qkv[:, :D], qkv[:, :D][:, hd], qkv[:, D:2 * D], qkv[:, D:2 * D][:, hd])):
            wqk[:, e, :, :, k] = chunks(w).reshape(P, DC, 2, P)
        wv[:, e] = chunks(qkv[:, 2 * D:])
        dense = f(f"L2_xattn_{x}_dense").reshape(4, 4, HD2, D)
        for h in range(4):
            wd[32 * h:32 * h + HD2, e] = dense[:, h].transpose(1, 0, 2)
        for k, n in enumerate(("gate", "up")):
            wgu[:, e, :, k, :FI] = chunks(f(f"L2_xattn_{x}_{n}"))
        wdn[e, :FI] = f(f"L2_xattn_{x}_down")
    o["wqk"], o["wv2"], o["wd"], o["wgu"] = wqk, wv, wd, wgu
    o["wdn"] = wdn.reshape(2, 6, P, D).transpose(2, 0, 1, 3)
    o["wcq"] = chunks(f("L2_xattn_cq_w"))
    o["wckv"] = f("L2_xattn_ckv_w").reshape(P, 2, P)
    cd = f("L2_xattn_cdense_w").reshape(4, 4, HC2, D)
    wcd = np.zeros((P, 4, D), np.float32)
    for h in range(4):
        wcd[32 * h:32 * h + HC2] = cd[:, h].transpose(1, 0, 2)
    o["wcd"] = wcd
    return o


def kernel(**inputs):
    import concourse.bacc as bacc
    from concourse.bass_utils import run_bass_kernel_spmd

    arrays = layouts(inputs)
    arrays.update(zip(_CONST, constants()))
    arrays = {f"in_{k}": np.ascontiguousarray(a) for k, a in arrays.items()}
    nc = bacc.Bacc("TRN2", target_bir_lowering=False, num_devices=1)
    io = {k[3:]: nc.dram_tensor(k, a.shape, mybir.dt.from_np(a.dtype), kind="ExternalInput").ap() for k, a in arrays.items()}
    io["out"] = nc.dram_tensor("out", (B, P, TT, D), F32, kind="ExternalOutput").ap()
    program(nc, io)
    r = run_bass_kernel_spmd(nc, [arrays], core_ids=[0])
    return r.results[0]["out"].transpose(0, 2, 1, 3).reshape(B, NT, D)
```
